# Optimizing a Trainium2 kernel written in Bass

```python
import numpy as np
import jax
import jax.numpy as jnp

def _softmax(x, axis=-1):
    return jax.nn.softmax(x, axis=axis)

def _gelu(x):
    return jax.nn.gelu(x, approximate=True)

def _silu(x):
    return jax.nn.silu(x)

def _sigmoid(x):
    return jax.nn.sigmoid(x)

def _layernorm(x, axis=-1, eps=1e-05):
    m = jnp.mean(x, axis=axis, keepdims=True)
    v = jnp.var(x, axis=axis, keepdims=True)
    return (x - m) / jnp.sqrt(v + eps)

def _scatter_add(tgt, idx, src, axis=0):
    return tgt.at[idx].add(src)

def _segment_sum(src, seg, n):
    return jax.ops.segment_sum(src, seg, n)
kernel_name = 'mk_gnn_preln_d4_gnn_r8_c6eebd'

def setup_inputs(seed: int=0):
    np.random.seed(seed)
    _w = jnp.asarray

    def _rec_inputs():
        import jax
        import jax.numpy as jnp
        _gk = jax.random.key(seed)
        x = -0.000202 + 1 * jax.random.normal(jax.random.fold_in(_gk, 1), (12500, 64), jnp.float32)
        src = jax.random.randint(jax.random.fold_in(_gk, 2), (200000,), 0, 12500, jnp.int32)
        dst = jnp.minimum((12500 * jax.random.uniform(jax.random.fold_in(_gk, 3), (200000,)) ** 2.0).astype(jnp.int32), 99999)
        _o = jnp.argsort(dst, stable=True)
        src = src[_o]
        dst = dst[_o]
        edge_type_4 = jax.random.randint(jax.random.fold_in(_gk, 13), (200000,), 0, 4, jnp.int32)
        edge_weight = jax.random.uniform(jax.random.fold_in(_gk, 14), (200000,), jnp.float32, 0.0, 0.999999)
        return (x, src, dst, edge_type_4, edge_weight)
    x, src, dst, edge_type_4, edge_weight = _rec_inputs()

    def _L0_gnn_setup():
        import jax, jax.numpy as jnp
        import numpy as np
        N_NODES = 12500
        N_EDGES = 200000
        DIM = 64
        key = jax.random.key(seed)
        ks = jax.random.split(key, 5)
        x = jax.random.normal(ks[0], (N_NODES, DIM), dtype=jnp.float32)
        edge_index = jax.random.randint(ks[1], (2, N_EDGES), 0, N_NODES, dtype=jnp.int64)
        scale = 1.0 / np.sqrt(DIM)
        W1 = jax.random.normal(ks[2], (DIM, DIM), dtype=jnp.float32) * scale
        b1 = jnp.zeros((DIM,), dtype=jnp.float32)
        W2 = jax.random.normal(ks[3], (DIM, DIM), dtype=jnp.float32) * scale
        b2 = jnp.zeros((DIM,), dtype=jnp.float32)
        return {'x': x, 'edge_index': edge_index, 'W1': W1, 'b1': b1, 'W2': W2, 'b2': b2}
    _L0_gnn_all = _L0_gnn_setup()
    _L0_gnn_in = {k: v for k, v in _L0_gnn_all.items() if k in ('W1', 'b1', 'W2', 'b2')}
    del _L0_gnn_all

    def _L1_gnn_setup():
        import jax, jax.numpy as jnp
        import numpy as np
        N = 6250
        E = 100000
        H = 64
        K = 4
        STEPS = 4

        def _gru_cell(a, feat, w_ih, w_hh, b_ih, b_hh):
            gi = a @ w_ih.T + b_ih
            gh = feat @ w_hh.T + b_hh
            i_r, i_z, i_n = jnp.split(gi, 3, axis=-1)
            h_r, h_z, h_n = jnp.split(gh, 3, axis=-1)
            r = jax.nn.sigmoid(i_r + h_r)
            z = jax.nn.sigmoid(i_z + h_z)
            n = jnp.tanh(i_n + r * h_n)
            return (1.0 - z) * n + z * feat
        key = jax.random.key(seed)
        ks = jax.random.split(key, 10)
        s = 0.05
        return {'h': jax.random.normal(ks[0], (N, H), jnp.float32), 'W': jax.random.normal(ks[1], (K, H, H), jnp.float32) * s, 'b': jax.random.normal(ks[2], (K, H), jnp.float32) * s, 'w_ih': jax.random.normal(ks[3], (3 * H, H), jnp.float32) * s, 'w_hh': jax.random.normal(ks[4], (3 * H, H), jnp.float32) * s, 'b_ih': jax.random.normal(ks[5], (3 * H,), jnp.float32) * s, 'b_hh': jax.random.normal(ks[6], (3 * H,), jnp.float32) * s, 'src': jax.random.randint(ks[7], (E,), 0, N, dtype=jnp.int32), 'dst': jax.random.randint(ks[8], (E,), 0, N, dtype=jnp.int32), 'etypes': jax.random.randint(ks[9], (E,), 0, K, dtype=jnp.int32)}
    _L1_gnn_all = _L1_gnn_setup()
    _L1_gnn_in = {k: v for k, v in _L1_gnn_all.items() if k in ('W', 'b', 'w_ih', 'w_hh', 'b_ih', 'b_hh')}
    del _L1_gnn_all

    def _L2_gnn_setup():
        import jax, jax.numpy as jnp
        import numpy as np
        N_NODES = 12500
        N_EDGES = 156250
        DIM = 64

        def _gcn_norm(edge_index, num_nodes):
            loop = jnp.arange(num_nodes, dtype=edge_index.dtype)
            row = jnp.concatenate([edge_index[0], loop])
            col = jnp.concatenate([edge_index[1], loop])
            w = jnp.ones(row.shape[0], dtype=jnp.float32)
            deg = jax.ops.segment_sum(w, col, num_segments=num_nodes)
            dinv = jnp.where(deg > 0, jax.lax.rsqrt(deg), 0.0)
            norm = dinv[row] * dinv[col]
            return (row, col, norm)

        def _gcn_conv(h, row, col, norm, W, b, num_nodes):
            h = h @ W
            msg = h[row] * norm[:, None]
            out = jax.ops.segment_sum(msg, col, num_segments=num_nodes)
            return out + b
        key = jax.random.key(seed)
        ks = jax.random.split(key, 7)
        x = jax.random.normal(ks[0], (N_NODES, DIM), dtype=jnp.float32)
        edge_index = jax.random.randint(ks[1], (2, N_EDGES), 0, N_NODES, dtype=jnp.int64)
        edge_weight = jax.random.uniform(ks[2], (N_EDGES,), dtype=jnp.float32)
        s = 1.0 / np.sqrt(DIM)
        W1 = jax.random.uniform(ks[3], (DIM, DIM), dtype=jnp.float32, minval=-s, maxval=s)
        b1 = jnp.zeros((DIM,), dtype=jnp.float32)
        W2 = jax.random.uniform(ks[4], (DIM, DIM), dtype=jnp.float32, minval=-s, maxval=s)
        b2 = jnp.zeros((DIM,), dtype=jnp.float32)
        return {'x': x, 'edge_index': edge_index, 'edge_weight': edge_weight, 'W1': W1, 'b1': b1, 'W2': W2, 'b2': b2}
    _L2_gnn_all = _L2_gnn_setup()
    _L2_gnn_in = {k: v for k, v in _L2_gnn_all.items() if k in ('W1', 'b1', 'W2', 'b2')}
    del _L2_gnn_all

    def _L3_gnn_setup():
        import jax, jax.numpy as jnp
        import numpy as np
        NEG_SLOPE = 0.3
        BN_EPS = 1e-05
        key = jax.random.key(seed)
        k1, k2, k3, k4 = jax.random.split(key, 4)
        N, E, IN_DIM, OUT_DIM = (6250, 100000, 64, 64)
        feature = jax.random.normal(k1, (N, IN_DIM), dtype=jnp.float32)
        edge_index = jax.random.randint(k2, (2, E), 0, N, dtype=jnp.int64)
        lim = 1.0 / np.sqrt(2 * IN_DIM)
        W = jax.random.uniform(k3, (OUT_DIM, 2 * IN_DIM), minval=-lim, maxval=lim, dtype=jnp.float32)
        b = jax.random.uniform(k4, (OUT_DIM,), minval=-lim, maxval=lim, dtype=jnp.float32)
        gamma = jnp.ones((OUT_DIM,), dtype=jnp.float32)
        beta = jnp.zeros((OUT_DIM,), dtype=jnp.float32)
        return {'feature': feature, 'edge_index': edge_index, 'W': W, 'b': b, 'gamma': gamma, 'beta': beta}
    _L3_gnn_all = _L3_gnn_setup()
    _L3_gnn_in = {k: v for k, v in _L3_gnn_all.items() if k in ('W', 'b', 'gamma', 'beta')}
    del _L3_gnn_all
    return {'x': x, 'src': src, 'dst': dst, 'edge_type_4': edge_type_4, 'edge_weight': edge_weight, 'L0_gnn_W1': _L0_gnn_in['W1'], 'L0_gnn_b1': _L0_gnn_in['b1'], 'L0_gnn_W2': _L0_gnn_in['W2'], 'L0_gnn_b2': _L0_gnn_in['b2'], 'L1_gnn_W': _L1_gnn_in['W'], 'L1_gnn_b': _L1_gnn_in['b'], 'L1_gnn_w_ih': _L1_gnn_in['w_ih'], 'L1_gnn_w_hh': _L1_gnn_in['w_hh'], 'L1_gnn_b_ih': _L1_gnn_in['b_ih'], 'L1_gnn_b_hh': _L1_gnn_in['b_hh'], 'L2_gnn_W1': _L2_gnn_in['W1'], 'L2_gnn_b1': _L2_gnn_in['b1'], 'L2_gnn_W2': _L2_gnn_in['W2'], 'L2_gnn_b2': _L2_gnn_in['b2'], 'L3_gnn_W': _L3_gnn_in['W'], 'L3_gnn_b': _L3_gnn_in['b'], 'L3_gnn_gamma': _L3_gnn_in['gamma'], 'L3_gnn_beta': _L3_gnn_in['beta']}

def reference(x, src, dst, edge_type_4, edge_weight, L0_gnn_W1, L0_gnn_b1, L0_gnn_W2, L0_gnn_b2, L1_gnn_W, L1_gnn_b, L1_gnn_w_ih, L1_gnn_w_hh, L1_gnn_b_ih, L1_gnn_b_hh, L2_gnn_W1, L2_gnn_b1, L2_gnn_W2, L2_gnn_b2, L3_gnn_W, L3_gnn_b, L3_gnn_gamma, L3_gnn_beta):
    import jax
    import jax.numpy as jnp

    def _L0_gnn_ref(x, edge_index, W1, b1, W2, b2):
        import jax, jax.numpy as jnp
        import numpy as np
        N_NODES = 12500
        N_EDGES = 200000
        DIM = 64
        src, dst = (edge_index[0], edge_index[1])
        msg = jax.nn.relu(x[src])
        agg = jax.ops.segment_sum(msg, dst, num_segments=x.shape[0])
        h = (1.0 + 0.0) * x + agg
        h = jax.nn.relu(h @ W1 + b1) @ W2 + b2
        return jax.nn.relu(h)

    def _L1_gnn_ref(h, W, b, w_ih, w_hh, b_ih, b_hh, src, dst, etypes):
        import jax, jax.numpy as jnp
        import numpy as np
        N = 6250
        E = 100000
        H = 64
        K = 4
        STEPS = 4

        def _gru_cell(a, feat, w_ih, w_hh, b_ih, b_hh):
            gi = a @ w_ih.T + b_ih
            gh = feat @ w_hh.T + b_hh
            i_r, i_z, i_n = jnp.split(gi, 3, axis=-1)
            h_r, h_z, h_n = jnp.split(gh, 3, axis=-1)
            r = jax.nn.sigmoid(i_r + h_r)
            z = jax.nn.sigmoid(i_z + h_z)
            n = jnp.tanh(i_n + r * h_n)
            return (1.0 - z) * n + z * feat
        num_nodes = h.shape[0]

        def step(feat, _):
            transformed = jnp.einsum('nd,khd->knh', feat, W) + b[:, None, :]
            msgs = transformed[etypes, src]
            a = jax.ops.segment_sum(msgs, dst, num_segments=num_nodes)
            feat = _gru_cell(a, feat, w_ih, w_hh, b_ih, b_hh)
            return (feat, None)
        feat, _ = jax.lax.scan(step, h, None, length=STEPS)
        return feat

    def _L2_gnn_ref(x, edge_index, edge_weight, W1, b1, W2, b2):
        import jax, jax.numpy as jnp
        import numpy as np
        N_NODES = 12500
        N_EDGES = 156250
        DIM = 64

        def _gcn_norm(edge_index, num_nodes):
            loop = jnp.arange(num_nodes, dtype=edge_index.dtype)
            row = jnp.concatenate([edge_index[0], loop])
            col = jnp.concatenate([edge_index[1], loop])
            w = jnp.ones(row.shape[0], dtype=jnp.float32)
            deg = jax.ops.segment_sum(w, col, num_segments=num_nodes)
            dinv = jnp.where(deg > 0, jax.lax.rsqrt(deg), 0.0)
            norm = dinv[row] * dinv[col]
            return (row, col, norm)

        def _gcn_conv(h, row, col, norm, W, b, num_nodes):
            h = h @ W
            msg = h[row] * norm[:, None]
            out = jax.ops.segment_sum(msg, col, num_segments=num_nodes)
            return out + b
        n = x.shape[0]
        row, col, norm = _gcn_norm(edge_index, n)
        h = _gcn_conv(x, row, col, norm, W1, b1, n)
        h = jax.nn.relu(h)
        out = _gcn_conv(h, row, col, norm, W2, b2, n)
        return out

    def _L3_gnn_ref(feature, edge_index, W, b, gamma, beta):
        import jax, jax.numpy as jnp
        import numpy as np
        NEG_SLOPE = 0.3
        BN_EPS = 1e-05
        N = feature.shape[0]
        src, dst = (edge_index[0], edge_index[1])
        x_i = feature[dst]
        x_j = feature[src]
        msg_in = jnp.concatenate([x_i, x_j - x_i], axis=-1)
        h = msg_in @ W.T + b
        mean = jnp.mean(h, axis=0)
        var = jnp.var(h, axis=0)
        h = (h - mean) * jax.lax.rsqrt(var + BN_EPS) * gamma + beta
        h = jnp.where(h >= 0, h, NEG_SLOPE * h)
        summed = jax.ops.segment_sum(h, dst, num_segments=N)
        counts = jax.ops.segment_sum(jnp.ones((h.shape[0],), h.dtype), dst, num_segments=N)
        return summed / jnp.maximum(counts, 1.0)[:, None]
    edge_index = jnp.stack([src, dst])
    h = jnp.maximum(_layernorm(x, axis=-1), 0.0)
    x = x + _L0_gnn_ref(h, edge_index, L0_gnn_W1, L0_gnn_b1, L0_gnn_W2, L0_gnn_b2)
    h = jnp.maximum(_layernorm(x, axis=-1), 0.0)
    x = x + _L1_gnn_ref(h, L1_gnn_W, L1_gnn_b, L1_gnn_w_ih, L1_gnn_w_hh, L1_gnn_b_ih, L1_gnn_b_hh, src, dst, edge_type_4)
    h = jnp.maximum(_layernorm(x, axis=-1), 0.0)
    x = x + _L2_gnn_ref(h, edge_index, edge_weight, L2_gnn_W1, L2_gnn_b1, L2_gnn_W2, L2_gnn_b2)
    h = jnp.maximum(_layernorm(x, axis=-1), 0.0)
    x = x + _L3_gnn_ref(h, edge_index, L3_gnn_W, L3_gnn_b, L3_gnn_gamma, L3_gnn_beta)
    return x

_drawn_inputs = setup_inputs


def setup_inputs(seed=0):
    import zlib

    import numpy as np

    out = dict(_drawn_inputs(seed))
    spreads = {'L0_gnn_b1': (0.0, 0.8),
     'L0_gnn_b2': (0.0, 0.8),
     'L2_gnn_b1': (0.0, 0.8),
     'L2_gnn_b2': (0.0, 0.613),
     'L3_gnn_gamma': (1.0, 0.6),
     'L3_gnn_beta': (0.0, 0.8)}
    factors = {'L1_gnn_w_hh': 4.212,
     'L1_gnn_b_ih': 8.0,
     'L1_gnn_b_hh': 8.0,
     'L2_gnn_W1': 2.731,
     'L3_gnn_b': 64.0,
     'L1_gnn_b': 2.875}
    for name, (base, spread) in spreads.items():
        noise = np.random.default_rng([zlib.crc32(name.encode()), seed]).standard_normal(out[name].shape)
        drawn = base * np.exp(spread * noise) if base else spread * noise
        out[name] = jnp.asarray(drawn.astype(out[name].dtype))
    for name, factor in factors.items():
        out[name] = (out[name] * factor).astype(out[name].dtype)
    return out
```

```python
from contextlib import ExitStack

import concourse.bass as bass
from concourse import mybir

F32 = mybir.dt.float32
I32 = mybir.dt.int32
ALU = mybir.AluOpType
ACT = mybir.ActivationFunctionType
AX_X = mybir.AxisListType.X

P = 128
N = 12500
E = 200000
D = 64
TYPES = 4
STEPS = 4
SLOPE = 0.3
EPS = 1e-5
NB = -(-N // P)
ROWS = -(-E // P)
VISITS = ROWS - 1 + NB
GRP = 10
TRIPS = VISITS // (2 * GRP)
VT = -(-VISITS // P)
CH = 2
NCH = NB // CH
ST_CH = 14
VK = VISITS + 1
LAST_PASS = 1 + STEPS + 2
RUN_MLP, RUN_TYPE, RUN_GRU, RUN_GCN, RUN_EDGE = 0, 1, 2, 1 + 2 * STEPS, 3 + 2 * STEPS
GRU_DVE = 5
LOADS = 21
S_SUM, S_SQ, S_MEAN, S_VAR, S_ROOT, S_SCALE, S_TMP = 0, 1, 2, 3, 4, 5, 6
EP, EF = 125, E // 125
SLOT_DMAS = [16 * (NCH // 2 + 1), 16 * (NCH // 2)]
FAR = 1 << 20
assert VISITS == 2 * GRP * TRIPS and NCH * CH == NB and NCH % 2 == 1


def gnn_kernel(nc, x, edges, dst, L0_W1, L0_b1, L0_W2, L0_b2, L1_Wt, L1_b, L1_wih, L1_whh, L1_bih, L1_bhh,
               L2_W1, L2_b1, L2_W2, L2_b2, L3_Wt, L3_b, L3_gamma, L3_beta, out):
    def dram(name, shape, dt):
        return nc.dram_tensor(name, shape, dt).ap()

    tab_gin = dram("tab_gin", [P * NB, D], F32)
    tab_gated = dram("tab_gated", [P * NB * TYPES, D], F32)
    tab_gcn = [dram(f"tab_gcn{i}", [P * NB, D], F32) for i in range(2)]
    tab_edge = dram("tab_edge", [P * NB, 2 * D], F32)
    kept = dram("kept", [P, VISITS, D], F32)
    blk_dram = dram("blk_dram", [VT, P], I32)

    with ExitStack() as ctx:
        def sb(name, shape, dt=F32):
            return ctx.enter_context(nc.sbuf_tensor(name, shape, dt))

        def sem(name):
            return ctx.enter_context(nc.semaphore(name))

        ps = ctx.enter_context(nc.psum_tensor("ps", [P, 4096], F32))

        X = sb("X", [P, NB, D])
        H = sb("H", [P, NB, D])
        A = sb("A", [P, NB * P])
        A3 = A[:, :].rearrange("p (b f) -> p b f", f=P)
        SUMS, FEAT = A3[:, :, 0:D], A3[:, :, D:P]
        DLOC = sb("DLOC", [P, VT * P])
        IDX = sb("IDX", [P, VT * P], I32)
        IDX4 = sb("IDX4", [P, VT * P], I32)
        BLK = sb("BLK", [1, VT * P], I32)
        STG = sb("STG", [P, 2, GRP], I32)
        G = sb("G", [P, 2, GRP, P])
        OH = sb("OH", [P, 2, GRP, P])
        CNT = sb("CNT", [P, NB])
        DINV = sb("DINV", [P, NB])
        SA = sb("SA", [P, NB])
        SB = sb("SB", [P, NB])
        SC = sb("SC", [P, NB])
        IDENT = sb("IDENT", [P, P])
        IOTAR = sb("IOTAR", [P, P])
        VIS = sb("VIS", [P, VT])
        BND = sb("BND", [P, NB])
        BNDH = sb("BNDH", [P, NB])
        CNTB = sb("CNTB", [P, NB])
        TOT = sb("TOT", [P, NB], I32)
        TS = sb("TS", [P, NB])
        IOB = sb("IOB", [P, NB])
        BJ = sb("BJ", [P, VT])
        BJ128 = sb("BJ128", [P, VT])
        TJF = sb("TJF", [P, VT])
        TJ = sb("TJ", [P, VT], I32)
        BT = sb("BT", [VT, P], I32)
        ONES = sb("ONES", [P, P])
        EPSC = sb("EPSC", [P, 1])
        PICK = sb("PICK", [P, 2, CH, P])
        XT = sb("XT", [D + 1, 2, CH * P])
        XG = sb("XG", [P, 2, CH * P])
        R1 = sb("R1", [D + 1, 2, CH * P])
        RZ = sb("RZ", [P, 2, CH, P])
        NN = sb("NN", [P, 2, CH, D])
        DZ = sb("DZ", [P, 2, CH, D])
        TW = sb("TW", [P, 2, CH * TYPES * D])
        WG = sb("WG", [P, 4 * D])
        BG = sb("BG", [1, 3, 4 * D])
        WT = sb("WT", [D + 1, TYPES * D])
        W01 = sb("W01", [D, D])
        B01 = sb("B01", [D, 1])
        W02 = sb("W02", [D + 1, D])
        W2 = sb("W2", [D, 2, D])
        W3 = sb("W3", [D, 2, D])
        W3A = sb("W3A", [D, D])
        BC = sb("BC", [P, 5, D])
        ST = sb("ST", [P, 8, D])
        OTS = sb("OTS", [P, GRP, P])

        Af = A[:, :]
        Hf = H[:, :, :].rearrange("p b f -> p (b f)")
        n3 = VT * 3 * P
        EB = Af[:, 0:n3].bitcast(I32).rearrange("p (g k e) -> p g k e", g=VT, k=3)
        F3 = Af[:, n3:2 * n3].rearrange("p (k g e) -> p k g e", g=VT, k=3)
        SLO = Af[:, 2 * n3:2 * n3 + VT * P].bitcast(I32).rearrange("p (g e) -> p g e", g=VT)
        SHI = OH[:, :, :, :].rearrange("p a u e -> p (a u e)")[:, 0:VT * P].bitcast(I32).rearrange(
            "p (g e) -> p g e", g=VT)
        DSTC = Hf[0:EP, 0:EF].bitcast(I32)
        JUNKV = Hf[0:EP, EF:2 * EF]
        JUNKS = Hf[0:EP, 2 * EF:3 * EF]

        Gf = G[:, :, :, :].rearrange("p h u f -> p (h u f)")
        LOADED = Gf[:, 0:2 * GRP * D].rearrange("p (h u f) -> p h u f", h=2, u=GRP)
        SCALED = Gf[:, 2 * GRP * D:3 * GRP * D].rearrange("p (u f) -> p u f", u=GRP)
        ACTED = Gf[:, 3 * GRP * D:4 * GRP * D].rearrange("p (u f) -> p u f", u=GRP)

        M1 = Gf[:, 0:ST_CH * D].rearrange("p (b f) -> p b f", f=D)
        M2 = Gf[:, ST_CH * D:2 * ST_CH * D].rearrange("p (b f) -> p b f", f=D)

        ps_g = ps[:, 0:3072].rearrange("p (h u f) -> p h u f", h=2, f=P)
        ps_t = ps[:, 0:1024].rearrange("p (s f) -> p s f", s=2)
        ps_o = ps[:, 1024:2048].rearrange("p (s f) -> p s f", s=2)
        ps_u = ps[:, 1536:1536 + GRP * D].rearrange("p (u f) -> p u f", f=D)
        ps_s = ps[:, 2560:2560 + GRP * D].rearrange("p (u f) -> p u f", f=D)
        ps_m = ps[:, 2048:3072].rearrange("p (s f) -> p s f", s=2)


        ps_gate = ps_o.rearrange("p s (c f) -> p s c f", c=CH)
        ps_vu = ps_o[:, :, 0:CH * P].rearrange("p s (c f) -> p s c f", c=CH)
        ps_x = ps_o[:, :, 0:CH * D].rearrange("p s (c f) -> p s c f", c=CH)
        tw_v2 = TW[:, :, 0:CH * P].rearrange("p s (c f) -> p s c f", c=CH)

        dst_in, x_in, w_in = sem("dst_in"), sem("x_in"), sem("w_in")
        iota_done = sem("iota_done")
        dve_done = sem("dve_done")
        bounds_set = sem("bounds_set")
        below_v = sem("below_v")
        below_s = sem("below_s")
        totals = sem("totals")
        rows_known = sem("rows_known")
        rows_in = sem("rows_in")
        cols_done = sem("cols_done")
        turned = sem("turned")
        tabled = sem("tabled")
        blk_out, blk_in = sem("blk_out"), sem("blk_in")

        centred, squared = sem("centred"), sem("squared")
        varred, rooted = sem("varred"), sem("rooted")
        normed = sem("normed")

        staged = [sem(f"staged{h}") for h in range(2)]
        pool_go = sem("pool_go")
        pe_go = sem("pe_go")
        rows_gated = [sem(f"rows_gated{h}") for h in range(2)]
        rows_other = [sem(f"rows_other{h}") for h in range(2)]
        onehot = [sem(f"onehot{h}") for h in range(2)]
        product = [sem(f"product{h}") for h in range(2)]
        visit_added = sem("visit_added")
        table_out = sem("table_out")
        chunk_picked = sem("chunk_picked")
        chunk_turned = sem("chunk_turned")
        chunk_copied = sem("chunk_copied")
        chunk_made = sem("chunk_made")
        mlp_in = sem("mlp_in")
        mlp_mid, mlp_act = sem("mlp_mid"), sem("mlp_act")
        mlp_done = sem("mlp_done")
        typ_dve, typ_act = sem("typ_dve"), sem("typ_act")
        typ_out = [sem(f"typ_out{s}") for s in range(2)]
        gru_sig, gru_tanh, gru_dve = sem("gru_sig"), sem("gru_tanh"), sem("gru_dve")
        root_deg, gcn_done, gcn_in = sem("root_deg"), sem("gcn_done"), sem("gcn_in")
        edg_v, edg_sq, edg_u = sem("edg_v"), sem("edg_sq"), sem("edg_u")
        edg_out = [sem(f"edg_out{s}") for s in range(2)]
        kept_out = [sem(f"kept_out{h}") for h in range(2)]
        stat_part, stat_sum, stat_var, stat_root = (sem(f"stat_{n}") for n in ("part", "sum", "var", "root"))
        bn_ready = sem("bn_ready")
        kept_in = [sem(f"kept_in{h}") for h in range(2)]
        e_onehot, e_turned, e_copied, e_picked, e_scaled, e_summed, e_acted, e_product = (
            sem(f"e_{n}") for n in ("onehot", "turned", "copied", "picked", "scaled", "summed", "acted",
                                    "product"))
        result, stored = sem("result"), sem("stored")

        block = ctx.enter_context(nc.Block())

        def chunks(eng, body, ahead=None):
            if ahead is None:
                def ahead(c, s, i):
                    return None
            ahead(0, 0, 0)
            ahead(1, 1, 0)
            body(0, 0, 0)
            ahead(2, 0, 1)
            body(1, 1, 0)
            with eng.Fori(1, NCH // 2) as i:
                ahead(2 * i + 1, 1, i)
                body(2 * i, 0, i)
                ahead(2 * i + 2, 0, i + 1)
                body(2 * i + 1, 1, i)
            body(NCH - 1, 0, NCH // 2)

        def groups(eng, body):
            for h in range(2):
                body(0, h, True)
            with eng.Fori(1, TRIPS) as i:
                for h in range(2):
                    body(i, h, False)

        def groups_apart(eng, body):
            body(0, 0, 0)
            with eng.Fori(0, TRIPS - 1) as i:
                body(2 * i + 1, 1, i)
                body(2 * i + 2, 0, i + 1)
            body(2 * TRIPS - 1, 1, TRIPS - 1)

        def static(v, least=1):
            return not isinstance(v, int) or v >= least

        def group_cols(t, i, h):
            return t[:, bass.ds(i * (2 * GRP) + h * GRP, GRP)]

        def two(t, c):
            return t[:, bass.ds(c * CH, CH), :]

        def table_rows(t, r):
            return t.rearrange("(p c r) f -> p c (r f)", p=P, c=NCH)

        @block.sync
        def _(sp):
            sp.dma_start(DSTC, dst.rearrange("(p f) -> p f", p=EP)).then_inc(dst_in, 16)
            sp.dma_start(X[:, :, :], x).then_inc(x_in, 16)
            loads = [(W01[:, :], L0_W1), (B01[:, :], L0_b1.rearrange("(p a) -> p a", a=1)),
                     (W02[0:D, :], L0_W2), (W02[D:D + 1, :], L0_b2.rearrange("(a n) -> a n", a=1)),
                     (WT[0:D, :], L1_Wt), (WT[D:D + 1, :], L1_b),
                     (WG[0:D, 0:3 * D], L1_wih), (WG[D:P, 0:2 * D], L1_whh[:, 0:2 * D]),
                     (WG[D:P, 3 * D:4 * D], L1_whh[:, 2 * D:3 * D]),
                     (BG[:, 0, 0:3 * D], L1_bih), (BG[:, 1, 0:2 * D], L1_bhh[:, 0:2 * D]),
                     (BG[:, 1, 3 * D:4 * D], L1_bhh[:, 2 * D:3 * D]),
                     (W2[:, 0, :], L2_W1), (W2[:, 1, :], L2_W2),
                     (W3A[:, :], L3_Wt[0:D, :]), (W3[:, 0, :], L3_Wt[D:P, :])]
            loads += [(BC[:, k, :], r.partition_broadcast(P)) for k, r in
                      enumerate((L2_b1, L2_b2, L3_b, L3_gamma, L3_beta))]
            assert len(loads) == LOADS
            for o, i in loads:
                sp.dma_start(o, i).then_inc(w_in, 16)

            sp.wait_ge(tabled, 4)
            sp.dma_start(blk_dram, BT[:, :]).then_inc(blk_out, 16)
            sp.wait_ge(blk_out, 16)
            sp.dma_start(BLK[:, :], blk_dram.rearrange("g (a e) -> a (g e)", a=1)).then_inc(blk_in, 16)

            sp.wait_ge(normed, 1)
            sp.dma_start(tab_gin.rearrange("(p b) f -> p b f", p=P), H[:, :, :]).then_inc(table_out, 16)

            gated = table_rows(tab_gated, CH * TYPES)
            with sp.Fori(0, STEPS) as step:
                def send(c, s, i):
                    sp.wait_ge(typ_dve, step * NCH + c + 1)
                    sp.wait_ge(typ_act, step * NCH + c + 1)
                    sp.dma_start(gated[:, bass.ds(c, 1), :], TW[:, s:s + 1, :]).then_inc(typ_out[s], 16)
                chunks(sp, send)

            for k in range(2):
                sp.wait_ge(gcn_done, (k + 1) * NCH)
                sp.dma_start(tab_gcn[k].rearrange("(p b) f -> p b f", p=P), FEAT).then_inc(table_out, 16)

            edge = table_rows(tab_edge, CH)

            def send_edge(c, s, i):
                sp.wait_ge(edg_v, c + 1)
                sp.wait_ge(edg_sq, c + 1)
                sp.dma_start(edge[:, bass.ds(c, 1), :], TW[:, s:s + 1, 0:CH * 2 * D]).then_inc(edg_out[s], 16)
            chunks(sp, send_edge)

            def keep(i, h, first):
                sp.wait_ge(rows_other[h], 16 * GRP * (3 * TRIPS + i + 1))
                sp.dma_start(kept[:, bass.ds(i * (2 * GRP) + h * GRP, GRP), :],
                             G[:, h, :, 0:D]).then_inc(kept_out[h], 16)
            groups(sp, keep)
            for h in range(2):
                sp.wait_ge(kept_out[h], TRIPS * 16)

            sp.wait_ge(bn_ready, 1)

            def load_kept(i, h, first):
                if not first:
                    sp.wait_ge(e_scaled, 2 * i + h - 1)
                sp.dma_start(LOADED[:, h, :, :], kept[:, bass.ds(i * (2 * GRP) + h * GRP, GRP), :]
                             ).then_inc(kept_in[h], 16)
            groups(sp, load_kept)
            sp.wait_ge(result, 1)
            sp.dma_start(out, X[:, :, :]).then_inc(stored, 16)
            sp.wait_ge(stored, 16)

        @block.gpsimd
        def _(pool):
            kw = dict(allow_small_or_imprecise_dtypes=True)
            nc.gpsimd.iota(IOTAR[:, :], [[1, P]], base=0, channel_multiplier=0, **kw).then_inc(iota_done, 1)
            nc.gpsimd.iota(VIS[:, :], [[P, VT]], base=0, channel_multiplier=1, **kw).then_inc(iota_done, 1)
            nc.gpsimd.iota(BND[:, :], [[P, NB]], base=P, channel_multiplier=0, **kw).then_inc(iota_done, 1)
            nc.gpsimd.iota(IOB[:, :], [[1, NB]], base=1, channel_multiplier=0, **kw).then_inc(iota_done, 1)
            pool.wait_ge(rows_known, 1)
            for g in range(VT):
                nc.gpsimd.indirect_dma_start(
                    out=EB[:, g, :, :].rearrange("p k e -> p (k e)"), out_offset=None, in_=edges,
                    in_offset=bass.IndirectOffsetOnAxis(ap=TJ[:, g:g + 1], axis=0)).then_inc(rows_in, 16)

            def gather(n, table, width, rows):
                def body(i, h, first):
                    pool.wait_ge(staged[h], n * TRIPS + i + 1)
                    pool.sem_inc(pool_go, 1)
                    if width == 2 * D and not first:
                        pool.wait_ge(kept_out[h], i * 16)
                        pool.sem_inc(pool_go, 1)
                    for u in range(GRP):
                        nc.gpsimd.indirect_dma_start(
                            out=G[:, h, u, 0:width], out_offset=None, in_=table,
                            in_offset=bass.IndirectOffsetOnAxis(ap=STG[:, h, u:u + 1], axis=0)
                        ).then_inc(rows[h], 16)
                groups(pool, body)

            def pick(run, src, width):
                def body(c, s, i):
                    if static(i):
                        pool.wait_ge(chunk_turned, run * NCH + c - 1)
                        pool.sem_inc(pool_go, 1)
                    nc.gpsimd.tensor_copy(PICK[:, s, :, 0:width], two(src, c)).then_inc(chunk_picked, 1)
                chunks(pool, body)

            pool.wait_ge(table_out, 16)
            gather(0, tab_gin, D, rows_other)
            pool.wait_ge(mlp_in, 1)
            pick(RUN_MLP, H, D)
            with pool.Fori(0, STEPS) as step:
                pool.wait_ge(visit_added, (step + 1) * VK + 1)
                pool.sem_inc(pool_go, 1)
                pick(2 * step + RUN_TYPE, FEAT, D)
                for s in range(2):
                    pool.wait_ge(typ_out[s], (step + 1) * SLOT_DMAS[s])
                    pool.sem_inc(pool_go, 1)
                gather(step + 1, tab_gated, D, rows_gated)
                pool.wait_ge(visit_added, (step + 2) * VK)
                pool.sem_inc(pool_go, 1)
                pick(2 * step + RUN_GRU, A3, P)
            for k in range(2):
                pool.wait_ge(gcn_in, k + 1)
                pick(RUN_GCN + k, H, D)
                pool.wait_ge(table_out, 16 * (k + 2))
                gather(STEPS + 1 + k, tab_gcn[k], D, rows_other)
            pool.wait_ge(normed, 4)
            pick(RUN_EDGE, H, D)
            for s in range(2):
                pool.wait_ge(edg_out[s], SLOT_DMAS[s])
            gather(LAST_PASS, tab_edge, 2 * D, rows_other)

            scale = ST[:, S_SCALE:S_SCALE + 1, :].broadcast_to([P, GRP, D])
            pool.wait_ge(bn_ready, 1)

            def scale_rows(g, h, i):
                pool.wait_ge(kept_in[h], i * 16 + 16)
                pool.sem_inc(pool_go, 1)
                if static(g):
                    pool.wait_ge(e_acted, g)
                    pool.sem_inc(pool_go, 1)
                nc.gpsimd.tensor_tensor(SCALED, LOADED[:, h, :, :], scale, ALU.mult).then_inc(e_scaled, 1)
            groups_apart(pool, scale_rows)

        @block.scalar
        def _(act):
            act.wait_ge(dst_in, 16)
            act.wait_ge(bounds_set, 1)
            with act.Fori(0, NB // 2) as k:
                nc.scalar.activation(JUNKS, DSTC, ACT.Sign, bias=BNDH[0:EP, bass.ds(2 * k + 1, 1)], scale=-1.0,
                                     accum_out=CNTB[0:EP, bass.ds(2 * k + 1, 1)]).then_inc(below_s, 1)
                act.wait_ge(below_s, k + 1)

            for k, table in enumerate((DLOC, IDX, IDX4)):
                act.wait_ge(turned, k + 1)
                half = 2048 * (k % 2)
                nc.scalar.copy(table[:, :], ps[:, half:half + VT * P]).then_inc(tabled, 1)
            act.wait_ge(turned, 4)
            nc.scalar.copy(BT[:, :], ps[0:VT, 2048:2048 + P]).then_inc(tabled, 1)

            def norm(n):
                act.wait_ge(centred, n + 1)
                nc.scalar.activation(SUMS, H[:, :, :], ACT.Square).then_inc(squared, 1)
                act.wait_ge(varred, n + 1)
                nc.scalar.activation(SB[:, :], SA[:, :], ACT.Sqrt, bias=EPSC[:, 0:1], scale=1.0 / D
                                     ).then_inc(rooted, 1)

            def stage_indices(n, table):
                def body(i, h, first):
                    if not first:
                        act.wait_ge(product[h], n * TRIPS + i)
                    nc.scalar.copy(STG[:, h, :], group_cols(table, i, h)).then_inc(staged[h], 1)
                groups(act, body)

            norm(0)
            act.wait_ge(tabled, 4)
            stage_indices(0, IDX)

            def copy_chunk(run, dst, rows, c, s):
                act.wait_ge(chunk_turned, run * NCH + c + 1)
                nc.scalar.copy(dst[0:rows, s, :], ps_t[0:rows, s, 0:CH * P]).then_inc(chunk_copied, 1)

            def mlp_chunk(c, s, i):
                copy_chunk(RUN_MLP, XT, D, c, s)
                act.wait_ge(mlp_mid, c + 1)
                nc.scalar.activation(R1[0:D, s, :], ps_m[0:D, s, 0:CH * P], ACT.Relu, bias=B01[:, 0:1]
                                     ).then_inc(mlp_act, 1)
            chunks(act, mlp_chunk)

            norm(1)

            with act.Fori(0, STEPS) as step:
                def type_chunk(c, s, i):
                    run = 2 * step + RUN_TYPE
                    copy_chunk(run, XT, D, c, s)
                    act.wait_ge(chunk_made, run * NCH + c + 1)
                    if static(i):
                        act.wait_ge(typ_out[s], step * SLOT_DMAS[s] + i * 16)
                    nc.scalar.copy(TW[:, s, 0:TYPES * D], ps_o[:, s, 0:TYPES * D]).then_inc(typ_act, 1)
                chunks(act, type_chunk)
                stage_indices(step + 1, IDX4)

                def gru_chunk(c, s, i):
                    run = 2 * step + RUN_GRU
                    copy_chunk(run, XG, P, c, s)
                    act.wait_ge(chunk_made, run * NCH + c + 1)
                    nc.scalar.activation(RZ[:, s, :, :], ps_gate[:, s, :, 0:2 * D], ACT.Sigmoid).then_inc(gru_sig, 1)
                    act.wait_ge(gru_dve, (step * NCH + c) * GRU_DVE + 2)
                    nc.scalar.activation(NN[:, s, :, :], NN[:, s, :, :], ACT.Tanh).then_inc(gru_tanh, 1)
                chunks(act, gru_chunk)

            act.wait_ge(normed, 2)
            nc.scalar.activation(SC[:, :], CNT[:, :], ACT.Sqrt, bias=ONES[:, 0:1]).then_inc(root_deg, 1)
            norm(2)
            for k in range(2):
                def gcn_chunk(c, s, i):
                    copy_chunk(RUN_GCN + k, XT, D, c, s)
                chunks(act, gcn_chunk)
                stage_indices(STEPS + 1 + k, IDX)

            norm(3)

            def edge_chunk(c, s, i):
                copy_chunk(RUN_EDGE, XT, D, c, s)
                act.wait_ge(edg_v, c + 1)
                nc.scalar.activation(tw_v2[:, s, :, D:P], tw_v2[:, s, :, 0:D], ACT.Square).then_inc(edg_sq, 1)
            chunks(act, edge_chunk)
            stage_indices(LAST_PASS, IDX)

            act.wait_ge(stat_var, 1)
            nc.scalar.activation(ST[:, S_ROOT, :], ST[:, S_VAR, :], ACT.Sqrt, bias=EPSC[:, 0:1]).then_inc(stat_root, 1)

            def edge_group(g, h, i):
                act.wait_ge(e_turned, g + 1)
                nc.scalar.copy(OTS[:, :, :].rearrange("p u e -> p (u e)"), ps[:, 0:GRP * P]).then_inc(e_copied, 1)
            groups_apart(act, edge_group)

        @block.tensor
        def _(pe):
            pe.wait_ge(below_v, NB // 2)
            pe.wait_ge(below_s, NB // 2)
            nc.tensor.matmul(ps[:, 0:NB], ONES[0:EP, :], CNTB[0:EP, :], start=True, stop=True).then_inc(totals, 1)

            pe.wait_ge(cols_done, 1)
            for k in range(3):
                if k == 2:
                    pe.wait_ge(tabled, 1)
                half = 2048 * (k % 2)
                for g in range(VT):
                    ins = nc.tensor.transpose(ps[:, half + g * P:half + (g + 1) * P], F3[:, k, g, :], IDENT[:, :])
                ins.then_inc(turned, 1)
            pe.wait_ge(tabled, 2)
            nc.tensor.transpose(ps[0:VT, 2048:2048 + P], BJ128[:, :], IDENT[:, :]).then_inc(turned, 1)

            def products(n, width, rows, m):
                def body(i, h, first):
                    pe.wait_ge(onehot[h], n * TRIPS + i + 1)
                    if not first:
                        pe.wait_ge(visit_added, n * VK + 1 + (2 * i + h - 1) * GRP)
                    pe.wait_ge(rows[h], (m * TRIPS + i + 1) * (16 * GRP))
                    for u in range(GRP):
                        ins = nc.tensor.matmul(ps_g[:, h, u, 0:width], OH[:, h, u, :], G[:, h, u, 0:width],
                                               start=True, stop=True)
                    ins.then_inc(product[h], 1)
                groups(pe, body)

            def turn(run, width):
                def ahead(c, s, i):
                    pe.wait_ge(chunk_picked, run * NCH + c + 1)
                    pe.sem_inc(pe_go, 1)
                    for k in range(CH):
                        ins = nc.tensor.transpose(ps_t[0:width, s, k * P:(k + 1) * P], PICK[:, s, k, 0:width],
                                                  IDENT[:, :])
                    ins.then_inc(chunk_turned, 1)
                return ahead

            pe.wait_ge(tabled, 4)
            products(0, D + 1, rows_other, 0)

            pe.wait_ge(w_in, 16 * LOADS)
            pe.wait_ge(mlp_in, 1)

            def mlp_chunk(c, s, i):
                pe.wait_ge(chunk_copied, RUN_MLP * NCH + c + 1)
                pe.sem_inc(pe_go, 1)
                nc.tensor.matmul(ps_m[0:D, s, 0:CH * P], W01[:, :], XT[0:D, s, :], start=True, stop=True
                                 ).then_inc(mlp_mid, 1)
                pe.wait_ge(mlp_act, c + 1)
                if static(i):
                    pe.wait_ge(mlp_done, c - 1)
                for k in range(CH):
                    ins = nc.tensor.matmul(ps_x[:, s, k, :], R1[:, s, k * P:(k + 1) * P], W02[:, :],
                                           start=True, stop=True)
                ins.then_inc(chunk_made, 1)
            chunks(pe, mlp_chunk, turn(RUN_MLP, D))

            with pe.Fori(0, STEPS) as step:
                def type_chunk(c, s, i):
                    pe.wait_ge(chunk_copied, (2 * step + RUN_TYPE) * NCH + c + 1)
                    if static(i):
                        pe.wait_ge(typ_dve, step * NCH + c - 1)
                        pe.wait_ge(typ_act, step * NCH + c - 1)
                    for k, bank in enumerate((ps_o, ps_m)):
                        ins = nc.tensor.matmul(bank[:, s, 0:TYPES * D], XT[:, s, k * P:(k + 1) * P], WT[:, :],
                                               start=True, stop=True)
                    ins.then_inc(chunk_made, 1)
                chunks(pe, type_chunk, turn(2 * step + RUN_TYPE, D))
                pe.wait_ge(typ_dve, (step + 1) * NCH)
                pe.wait_ge(typ_act, (step + 1) * NCH)
                products(step + 1, D, rows_gated, step)

                pe.wait_ge(visit_added, (step + 2) * VK)

                def gru_chunk(c, s, i):
                    pe.wait_ge(chunk_copied, (2 * step + RUN_GRU) * NCH + c + 1)
                    if static(i):
                        pe.wait_ge(gru_dve, (step * NCH + c - 2) * GRU_DVE + 2)
                    for k in range(CH):
                        nc.tensor.matmul(ps_gate[:, s, k, :], XG[:, s, k * P:(k + 1) * P], WG[:, :],
                                         start=True, stop=False)
                        ins = nc.tensor.matmul(ps_gate[:, s, k, :], ONES[0:1, :], BG[0:1, 2, :],
                                               start=False, stop=True)
                    ins.then_inc(chunk_made, 1)
                chunks(pe, gru_chunk, turn(2 * step + RUN_GRU, P))
                pe.wait_ge(gru_dve, (step + 1) * (NCH * GRU_DVE))

            for n in range(2):
                def gcn_chunk(c, s, i):
                    pe.wait_ge(chunk_copied, (RUN_GCN + n) * NCH + c + 1)
                    if static(i):
                        pe.wait_ge(gcn_done, n * NCH + c - 1)
                    for k in range(CH):
                        ins = nc.tensor.matmul(ps_x[:, s, k, :], XT[0:D, s, k * P:(k + 1) * P], W2[:, n, :],
                                               start=True, stop=True)
                    ins.then_inc(chunk_made, 1)
                chunks(pe, gcn_chunk, turn(RUN_GCN + n, D))
                pe.wait_ge(gcn_done, (n + 1) * NCH)
                products(STEPS + 1 + n, D, rows_other, 1 + n)
                pe.wait_ge(visit_added, (STEPS + 2 + n) * VK)

            def edge_chunk(c, s, i):
                pe.wait_ge(chunk_copied, RUN_EDGE * NCH + c + 1)
                if static(i):
                    pe.wait_ge(edg_u, c - 1)
                for k in range(CH):
                    ins = nc.tensor.matmul(ps_vu[:, s, k, :], XT[0:D, s, k * P:(k + 1) * P],
                                           W3[:, :, :].rearrange("p a f -> p (a f)"), start=True, stop=True)
                ins.then_inc(chunk_made, 1)
            chunks(pe, edge_chunk, turn(RUN_EDGE, D))
            pe.wait_ge(edg_u, NCH)
            products(LAST_PASS, 2 * D, rows_other, 3)

            pe.wait_ge(stat_part, 1)
            nc.tensor.matmul(ps[:, 0:2 * D], ONES[:, :], ST[:, S_SUM:S_SQ + 1, :].rearrange("p a f -> p (a f)"),
                             start=True, stop=True).then_inc(stat_sum, 1)

            pe.wait_ge(bn_ready, 1)
            pe.wait_ge(blk_in, 16)

            def turn_group(g, h):
                pe.wait_ge(e_onehot, g + 1)
                for u in range(GRP):
                    ins = nc.tensor.transpose(ps[:, u * P:(u + 1) * P], OH[:, h, u, :], IDENT[:, :])
                ins.then_inc(e_turned, 1)

            def edge_group(g, h, i):
                pe.wait_ge(e_copied, g + 1)
                if static(g):
                    pe.wait_ge(e_summed, g)
                for u in range(GRP):
                    b = pe.value_load(BLK[0:1, bass.ds(g * GRP + u, 1)], min_val=0, max_val=(NB - 1) * P)
                    ins = nc.tensor.matmul(ps_u[:, u, :], OTS[:, u, :], A[:, bass.ds(b + D, D)],
                                           start=True, stop=True)
                ins.then_inc(e_picked, 1)
                if not isinstance(g, int) or g < 2 * TRIPS - 1:
                    turn_group(g + 1, 1 - h)
                pe.wait_ge(e_acted, g + 1)
                if static(g):
                    pe.wait_ge(visit_added, (LAST_PASS + 1) * VK + 1 + g * GRP)
                for u in range(GRP):
                    ins = nc.tensor.matmul(ps_s[:, u, :], OH[:, h, u, :], ACTED[:, u, :], start=True, stop=True)
                ins.then_inc(e_product, 1)
            turn_group(0, 0)
            groups_apart(pe, edge_group)

        @block.vector
        def _(dve):
            count = [0]

            def link(ins):
                count[0] += 1
                ins.then_inc(dve_done, 1)
                dve.wait_ge(dve_done, count[0])

            V = nc.vector

            V.memset(EPSC[:, :], EPS)
            V.memset(ONES[:, :], 1.0)
            V.memset(XT[D:D + 1, :, :], 1.0)
            V.memset(R1[D:D + 1, :, :], 1.0)
            V.memset(CNTB[:, :], 0.0)
            V.memset(WG[0:D, 3 * D:4 * D], 0.0)
            V.memset(WG[D:P, 2 * D:3 * D], 0.0)
            V.memset(BG[:, 0, 3 * D:4 * D], 0.0)
            V.memset(BG[:, 1, 2 * D:3 * D], 0.0)
            dve.wait_ge(iota_done, 4)
            V.tensor_scalar(IDENT[:, :], IOTAR[:, :], VIS[:, 0:1], None, ALU.is_equal)
            V.tensor_scalar(BNDH[:, :], BND[:, :], -0.5, None, ALU.add).then_inc(bounds_set, 1)

            dve.wait_ge(bounds_set, 1)
            dve.wait_ge(dst_in, 16)
            with dve.Fori(0, NB // 2) as k:
                V.tensor_scalar(JUNKV, DSTC, BND[0:EP, bass.ds(2 * k, 1)], 0.0, ALU.is_lt, ALU.add,
                                accum_out=CNTB[0:EP, bass.ds(2 * k, 1)]).then_inc(below_v, 1)
                dve.wait_ge(below_v, k + 1)

            dve.wait_ge(totals, 1)
            even = ps[:, 0:NB].rearrange("p (b two) -> p two b", two=2)
            to = TOT[:, :].rearrange("p (b two) -> p two b", two=2)
            link(V.tensor_copy(to[:, 0, :], even[:, 0, :]))
            link(V.tensor_scalar(to[:, 1, :], even[:, 1, :], 0.5, E / 2.0, ALU.mult, ALU.add))
            link(V.tensor_scalar(TOT[:, :], TOT[:, :], 7, None, ALU.arith_shift_right))
            link(V.tensor_tensor(TS[:, :], TOT[:, :], IOB[:, :], ALU.add))
            for g in range(VT):
                link(V.tensor_scalar(CNTB[:, 0:NB - 1], TS[:, 0:NB - 1], VIS[:, g:g + 1], 0.0, ALU.is_le, ALU.add,
                                     accum_out=BJ[:, g:g + 1]))
            link(V.tensor_tensor(TJF[:, :], VIS[:, :], BJ[:, :], ALU.subtract))
            V.tensor_scalar(TJ[:, :], TJF[:, :], float(ROWS - 1), None, ALU.min).then_inc(rows_known, 1)
            link(V.tensor_scalar(BJ128[:, :], BJ[:, :], float(P), None, ALU.mult))

            dve.wait_ge(rows_in, 16 * VT)
            for g in range(VT):
                V.tensor_scalar(F3[:, 0, g, :], EB[:, g, 0, :], BJ128[:, g:g + 1], None, ALU.subtract)
            V.tensor_scalar(SLO, EB[:, :, 1, :], P - 1, None, ALU.bitwise_and)
            link(V.tensor_scalar(SHI, EB[:, :, 1, :], 7, None, ALU.arith_shift_right))
            link(V.scalar_tensor_tensor(F3[:, 1, :, :], SLO, float(NB), SHI, ALU.mult, ALU.add))
            V.scalar_tensor_tensor(F3[:, 2, :, :], F3[:, 1, :, :], float(TYPES), EB[:, :, 2, :], ALU.mult, ALU.add
                                   ).then_inc(cols_done, 1)

            def over_f(t):
                return t[:, :].unsqueeze(2).broadcast_to([P, NB, D])

            def over_b(k):
                return BC[:, k:k + 1, :].broadcast_to([P, NB, D])

            def norm(n, to):
                link(V.tensor_reduce(SA[:, :], X[:, :, :], AX_X, ALU.add))
                link(V.tensor_scalar(SA[:, :], SA[:, :], -1.0 / D, None, ALU.mult))
                V.tensor_tensor(H[:, :, :], X[:, :, :], over_f(SA), ALU.add).then_inc(centred, 1)
                dve.wait_ge(squared, n + 1)
                V.tensor_reduce(SA[:, :], SUMS, AX_X, ALU.add).then_inc(varred, 1)
                dve.wait_ge(rooted, n + 1)
                link(V.reciprocal(SB[:, :], SB[:, :]))
                V.scalar_tensor_tensor(to, H[:, :, :], 0.0, over_f(SB), ALU.max, ALU.mult).then_inc(normed, 1)

            def clear(view):
                V.memset(view, 0.0).then_inc(visit_added, 1)

            def visit_blocks(v):
                return [dve.value_load(BLK[0:1, bass.ds(v + u, 1)], min_val=0, max_val=(NB - 1) * P)
                        for u in range(GRP)]

            def add_visits(n, v, at, products_, width):
                for u in range(GRP):
                    sums = A[:, bass.ds(at[u], width)]
                    dve.wait_ge(visit_added, n * VK + v + (u + 1))
                    V.tensor_tensor(sums, sums, products_[:, u, 0:width], ALU.add).then_inc(visit_added, 1)

            def onehots(cols, h):
                return V.tensor_tensor(OH[:, h, :, :], IOTAR[:, :].unsqueeze(1).broadcast_to([P, GRP, P]),
                                       cols.unsqueeze(2).broadcast_to([P, GRP, P]), ALU.is_equal)

            def sum_edges(n, width):
                for h in range(2):
                    onehots(group_cols(DLOC, 0, h), h).then_inc(onehot[h], 1)

                def add_group(i, h):
                    v = i * (2 * GRP) + h * GRP
                    at = visit_blocks(v)
                    dve.wait_ge(product[h], n * TRIPS + i + 1)
                    add_visits(n, v, at, ps_g[:, h, :, :], width)
                with dve.Fori(0, TRIPS - 1) as i:
                    for h in range(2):
                        add_group(i, h)
                        onehots(group_cols(DLOC, i + 1, h), h).then_inc(onehot[h], 1)
                for h in range(2):
                    add_group(TRIPS - 1, h)
                dve.wait_ge(visit_added, (n + 1) * VK)

            dve.wait_ge(x_in, 16)
            norm(0, H[:, :, :])
            V.memset(G[:, :, :, D:D + 1], 1.0)
            clear(A3[:, :, 0:D + 1])
            dve.wait_ge(tabled, 4)
            dve.wait_ge(blk_in, 16)
            sum_edges(0, D + 1)
            V.tensor_copy(CNT[:, :].unsqueeze(2), A3[:, :, D:D + 1])
            dve.wait_ge(table_out, 16)
            V.tensor_tensor(H[:, :, :], H[:, :, :], SUMS, ALU.add).then_inc(mlp_in, 1)

            def mlp_chunk(c, s, i):
                dve.wait_ge(chunk_made, RUN_MLP * NCH + c + 1)
                V.scalar_tensor_tensor(two(X, c), ps_x[:, s, :, :], 0.0, two(X, c), ALU.max, ALU.add
                                       ).then_inc(mlp_done, 1)
            chunks(dve, mlp_chunk)
            dve.wait_ge(mlp_done, NCH)

            link(V.tensor_tensor(BG[:, 2, :], BG[:, 0, :], BG[:, 1, :], ALU.add))
            norm(1, FEAT)
            with dve.Fori(0, STEPS) as step:
                clear(SUMS)

                def type_chunk(c, s, i):
                    dve.wait_ge(chunk_made, (2 * step + RUN_TYPE) * NCH + c + 1)
                    if static(i):
                        dve.wait_ge(typ_out[s], step * SLOT_DMAS[s] + i * 16)
                    V.tensor_copy(TW[:, s, TYPES * D:], ps_m[:, s, 0:TYPES * D]).then_inc(typ_dve, 1)
                chunks(dve, type_chunk)
                sum_edges(step + 1, D)

                def gru_chunk(c, s, i):
                    done = (step * NCH + c) * GRU_DVE
                    feat, z = two(FEAT, c), RZ[:, s, :, D:2 * D]
                    dve.wait_ge(gru_sig, step * NCH + c + 1)
                    V.tensor_tensor(NN[:, s, :, :], RZ[:, s, :, 0:D], ps_gate[:, s, :, 3 * D:4 * D], ALU.mult
                                    ).then_inc(gru_dve, 1)
                    dve.wait_ge(gru_dve, done + 1)
                    V.tensor_tensor(NN[:, s, :, :], NN[:, s, :, :], ps_gate[:, s, :, 2 * D:3 * D], ALU.add
                                    ).then_inc(gru_dve, 1)
                    dve.wait_ge(gru_tanh, step * NCH + c + 1)
                    V.tensor_tensor(DZ[:, s, :, :], feat, NN[:, s, :, :], ALU.subtract).then_inc(gru_dve, 1)
                    dve.wait_ge(gru_dve, done + 3)
                    V.tensor_tensor(DZ[:, s, :, :], DZ[:, s, :, :], z, ALU.mult).then_inc(gru_dve, 1)
                    dve.wait_ge(gru_dve, done + 4)
                    V.tensor_tensor(feat, NN[:, s, :, :], DZ[:, s, :, :], ALU.add).then_inc(gru_dve, 1)
                chunks(dve, gru_chunk)
                dve.wait_ge(gru_dve, (step + 1) * (NCH * GRU_DVE))
            link(V.tensor_tensor(X[:, :, :], X[:, :, :], FEAT, ALU.add))

            norm(2, H[:, :, :])
            dve.wait_ge(root_deg, 1)
            link(V.reciprocal(DINV[:, :], SC[:, :]))
            for k in range(2):
                clear(SUMS)
                dve.wait_ge(visit_added, (STEPS + 1 + k) * VK + 1)
                dve.sem_inc(gcn_in, 1)

                def gcn_chunk(c, s, i):
                    dve.wait_ge(chunk_made, (RUN_GCN + k) * NCH + c + 1)
                    scale = DINV[:, bass.ds(c * CH, CH)].unsqueeze(2).broadcast_to([P, CH, D])
                    V.tensor_tensor(two(FEAT, c), ps_x[:, s, :, :], scale, ALU.mult).then_inc(gcn_done, 1)
                chunks(dve, gcn_chunk)
                sum_edges(STEPS + 1 + k, D)
                link(V.tensor_tensor(H[:, :, :], SUMS, FEAT, ALU.add))
                link(V.tensor_tensor(H[:, :, :], H[:, :, :], over_f(DINV), ALU.mult))
                link(V.tensor_tensor(H[:, :, :], H[:, :, :], over_b(k), ALU.add))
                if k == 0:
                    link(V.tensor_scalar(H[:, :, :], H[:, :, :], 0.0, None, ALU.max))
                    dve.wait_ge(table_out, 32)
                else:
                    link(V.tensor_tensor(X[:, :, :], X[:, :, :], H[:, :, :], ALU.add))

            link(V.tensor_tensor(W3[:, 1, :], W3A[:, :], W3[:, 0, :], ALU.subtract))
            norm(3, H[:, :, :])
            clear(A3)

            def edge_chunk(c, s, i):
                dve.wait_ge(chunk_made, RUN_EDGE * NCH + c + 1)
                if static(i):
                    dve.wait_ge(edg_out[s], i * 16)
                V.tensor_copy(tw_v2[:, s, :, 0:D], ps_vu[:, s, :, 0:D]).then_inc(edg_v, 1)
                V.tensor_copy(two(H, c), ps_vu[:, s, :, D:P]).then_inc(edg_u, 1)
            chunks(dve, edge_chunk)
            sum_edges(LAST_PASS, 2 * D)

            link(V.memset(ST[:, S_SUM:S_SQ + 1, :], 0.0))
            for h in range(2):
                dve.wait_ge(kept_out[h], TRIPS * 16)
            for j in range(0, NB, ST_CH):
                u, s1, s2 = H[:, j:j + ST_CH, :], SUMS[:, j:j + ST_CH, :], FEAT[:, j:j + ST_CH, :]
                deg = CNT[:, j:j + ST_CH].unsqueeze(2).broadcast_to([P, ST_CH, D])
                link(V.tensor_tensor(M1, u, deg, ALU.mult))
                link(V.scalar_tensor_tensor(M2, s1, 2.0, M1, ALU.mult, ALU.add))
                link(V.tensor_tensor(M2, M2, u, ALU.mult))
                link(V.tensor_tensor(M2, M2, s2, ALU.add))
                link(V.tensor_tensor(M1, M1, s1, ALU.add))
                for m, row in ((M1, S_SUM), (M2, S_SQ)):
                    link(V.tensor_reduce(ST[:, S_TMP, :], m.rearrange("p b f -> p f b"), AX_X, ALU.add))
                    link(V.tensor_tensor(ST[:, row, :], ST[:, row, :], ST[:, S_TMP, :], ALU.add))
            dve.sem_inc(stat_part, 1)

            bias, gamma, beta = (BC[:, k, :] for k in (2, 3, 4))
            dve.wait_ge(stat_sum, 1)
            link(V.tensor_scalar(ST[:, S_MEAN, :], ps[:, 0:D], 1.0 / E, None, ALU.mult))
            link(V.tensor_scalar(ST[:, S_VAR, :], ps[:, D:2 * D], 1.0 / E, None, ALU.mult))
            link(V.tensor_tensor(ST[:, S_TMP, :], ST[:, S_MEAN, :], ST[:, S_MEAN, :], ALU.mult))
            link(V.tensor_tensor(ST[:, S_VAR, :], ST[:, S_VAR, :], ST[:, S_TMP, :], ALU.subtract))
            V.tensor_scalar(ST[:, S_VAR, :], ST[:, S_VAR, :], 0.0, None, ALU.max).then_inc(stat_var, 1)
            link(V.tensor_tensor(ST[:, S_MEAN, :], ST[:, S_MEAN, :], bias, ALU.add))
            dve.wait_ge(stat_root, 1)
            link(V.reciprocal(ST[:, S_SCALE, :], ST[:, S_ROOT, :]))
            link(V.tensor_tensor(ST[:, S_SCALE, :], ST[:, S_SCALE, :], gamma, ALU.mult))
            mean = ST[:, S_MEAN:S_MEAN + 1, :].broadcast_to([P, NB, D])
            scale = ST[:, S_SCALE:S_SCALE + 1, :].broadcast_to([P, NB, D])
            link(V.tensor_tensor(H[:, :, :], H[:, :, :], over_b(2), ALU.add))
            link(V.tensor_tensor(H[:, :, :], H[:, :, :], mean, ALU.subtract))
            link(V.tensor_tensor(H[:, :, :], H[:, :, :], scale, ALU.mult))
            link(V.tensor_tensor(FEAT, H[:, :, :], over_b(4), ALU.add))
            clear(SUMS)
            dve.wait_ge(visit_added, (LAST_PASS + 1) * VK + 1)
            dve.sem_inc(bn_ready, 1)

            def edge_onehots(g, h):
                onehots(DLOC[:, bass.ds(g * GRP, GRP)], h).then_inc(e_onehot, 1)

            def edge_sum(g, h):
                dve.wait_ge(e_picked, g + 1)
                dve.wait_ge(e_scaled, g + 1)
                V.tensor_tensor(SCALED, SCALED, ps_u, ALU.add).then_inc(e_summed, 1)
                dve.wait_ge(e_summed, g + 1)
                if static(g):
                    dve.wait_ge(e_product, g)
                V.scalar_tensor_tensor(ACTED, SCALED, SLOPE, SCALED, ALU.mult, ALU.max).then_inc(e_acted, 1)

            def add_edges(g):
                at = visit_blocks(g * GRP)
                dve.wait_ge(e_product, g + 1)
                add_visits(LAST_PASS + 1, g * GRP, at, ps_s, D)

            edge_onehots(0, 0)
            edge_sum(0, 0)
            edge_onehots(1, 1)
            with dve.Fori(0, TRIPS - 1) as i:
                for h in (1, 0):
                    g = 2 * i + (2 - h)
                    edge_sum(g, h)
                    add_edges(g - 1)
                    edge_onehots(g + 1, 1 - h)
            edge_sum(2 * TRIPS - 1, 1)
            add_edges(2 * TRIPS - 2)
            add_edges(2 * TRIPS - 1)
            dve.wait_ge(visit_added, (LAST_PASS + 2) * VK)

            link(V.tensor_scalar(CNT[:, :], CNT[:, :], 1.0, None, ALU.max))
            link(V.reciprocal(CNT[:, :], CNT[:, :]))
            link(V.tensor_tensor(H[:, :, :], SUMS, over_f(CNT), ALU.mult))
            V.tensor_tensor(X[:, :, :], X[:, :, :], H[:, :, :], ALU.add).then_inc(result, 1)


def kernel(**inputs):
    import numpy as np
    import concourse.bacc as bacc
    from concourse.bass_utils import run_bass_kernel_spmd

    a = {k: np.asarray(v) for k, v in inputs.items()}
    xp = np.zeros((NB * P, D), np.float32)
    xp[:N] = a["x"]
    edges = np.full((3, ROWS * P), 0, np.int32)
    edges[0, E:] = FAR
    for k, name in enumerate(("dst", "src", "edge_type_4")):
        edges[k, :E] = a[name]
    arrays = {
        "x": np.ascontiguousarray(xp.reshape(NB, P, D).transpose(1, 0, 2)),
        "edges": np.ascontiguousarray(edges.reshape(3, ROWS, P).transpose(1, 0, 2)).reshape(ROWS, 3 * P),
        "dst": a["dst"],
        "L0_W1": a["L0_gnn_W1"], "L0_b1": a["L0_gnn_b1"], "L0_W2": a["L0_gnn_W2"], "L0_b2": a["L0_gnn_b2"],
        "L1_Wt": a["L1_gnn_W"].transpose(2, 0, 1).reshape(D, TYPES * D), "L1_b": a["L1_gnn_b"].reshape(1, TYPES * D),
        "L1_wih": a["L1_gnn_w_ih"].T, "L1_whh": a["L1_gnn_w_hh"].T,
        "L1_bih": a["L1_gnn_b_ih"].reshape(1, 3 * D), "L1_bhh": a["L1_gnn_b_hh"].reshape(1, 3 * D),
        "L2_W1": a["L2_gnn_W1"], "L2_b1": a["L2_gnn_b1"], "L2_W2": a["L2_gnn_W2"], "L2_b2": a["L2_gnn_b2"],
        "L3_Wt": a["L3_gnn_W"].T, "L3_b": a["L3_gnn_b"], "L3_gamma": a["L3_gnn_gamma"], "L3_beta": a["L3_gnn_beta"],
    }
    arrays = {k: np.ascontiguousarray(v) for k, v in arrays.items()}
    nc = bacc.Bacc("TRN2", target_bir_lowering=False, num_devices=1)
    args = {k: nc.dram_tensor(k, v.shape, mybir.dt.from_np(v.dtype), kind="ExternalInput").ap()
            for k, v in arrays.items()}
    out = nc.dram_tensor("out", (P, NB, D), F32, kind="ExternalOutput").ap()
    gnn_kernel(nc, out=out, **args)
    r = run_bass_kernel_spmd(nc, [arrays], core_ids=[0])
    return r.results[0]["out"].transpose(1, 0, 2).reshape(NB * P, D)[:N]
```

```python
from contextlib import ExitStack

import concourse.bass as bass
from concourse import mybir

F32 = mybir.dt.float32
I32 = mybir.dt.int32
BF16 = mybir.dt.bfloat16
ALU = mybir.AluOpType
ACT = mybir.ActivationFunctionType
AX_X = mybir.AxisListType.X

P = 128
N = 12500
E = 200000
D = 64
TYPES = 4
STEPS = 4
SLOPE = 0.3
EPS = 1e-5
NB = -(-N // P)
ROWS = -(-E // P)
VISITS = ROWS - 1 + NB
GRP = 10
TRIPS = VISITS // (2 * GRP)
VT = -(-VISITS // P)
CH = 2
NCH = NB // CH
ST_CH = 14
GK = 2 * TRIPS + 1
QUADS = -(-GRP // 4)
LPG = 4 * QUADS
LAST_PASS = 1 + STEPS + 2
RUN_MLP, RUN_TYPE, RUN_GRU, RUN_GCN, RUN_EDGE = 0, 1, 2, 1 + 2 * STEPS, 3 + 2 * STEPS
LOADS = 21
S_SUM, S_SQ, S_MEAN, S_VAR, S_ROOT, S_SCALE, S_TMP = 0, 1, 2, 3, 4, 5, 6
EP, EF = 125, E // 125
SLOT_DMAS = [16 * (NCH // 2 + 1), 16 * (NCH // 2)]
FAR = 1 << 20
assert VISITS == 2 * GRP * TRIPS and NCH * CH == NB and NCH % 2 == 1


def gnn_kernel(nc, x, edges, dst, L0_W1, L0_b1, L0_W2, L0_b2, L1_Wt, L1_b, L1_wih, L1_whh, L1_bih, L1_bhh,
               L2_W1, L2_b1, L2_W2, L2_b2, L3_Wt, L3_b, L3_gamma, L3_beta, out):
    def dram(name, shape, dt):
        return nc.dram_tensor(name, shape, dt).ap()

    tab_gin = dram("tab_gin", [P * NB, D], F32)
    tab_gated = dram("tab_gated", [P * NB * TYPES, D], F32)
    tab_gcn = [dram(f"tab_gcn{i}", [P * NB, D], F32) for i in range(2)]
    tab_edge = dram("tab_edge", [P * NB, 2 * D], F32)
    kept = dram("kept", [P, VISITS, D], F32)
    blk_dram = dram("blk_dram", [VT, P], I32)
    dloc_dram = dram("dloc_dram", [VT * P, P], BF16)

    with ExitStack() as ctx:
        def sb(name, shape, dt=F32):
            return ctx.enter_context(nc.sbuf_tensor(name, shape, dt))

        def sem(name):
            return ctx.enter_context(nc.semaphore(name))

        ps = ctx.enter_context(nc.psum_tensor("ps", [P, 4096], F32))

        X = sb("X", [P, NB, D])
        H = sb("H", [P, NB, D])
        A = sb("A", [P, NB * P])
        A3 = A[:, :].rearrange("p (b f) -> p b f", f=P)
        SUMS, FEAT = A3[:, :, 0:D], A3[:, :, D:P]
        DLOC = sb("DLOC", [P, VT * P])
        IDX = sb("IDX", [P, VT * P], I32)
        IDX4 = sb("IDX4", [P, VT * P], I32)
        BLK = sb("BLK", [1, VT * P], I32)
        LOC = sb("LOC", [1, 2 * TRIPS * LPG], I32)
        FIRST = sb("FIRST", [1, 2 * TRIPS], I32)
        ZERO = sb("ZERO", [1, 512], BF16)
        STG = sb("STG", [P, 2, GRP], I32)
        G = sb("G", [P, 2, GRP, P])
        OH = sb("OH", [P, 2, GRP, P])
        CNT = sb("CNT", [P, NB])
        DINV = sb("DINV", [P, NB])
        SA = sb("SA", [P, NB])
        SB = sb("SB", [P, NB])
        SC = sb("SC", [P, NB])
        IDENT = sb("IDENT", [P, P])
        IOTAR = sb("IOTAR", [P, P])
        VIS = sb("VIS", [P, VT])
        BND = sb("BND", [P, NB])
        BNDH = sb("BNDH", [P, NB])
        CNTB = sb("CNTB", [P, NB])
        TOT = sb("TOT", [P, NB], I32)
        TS = sb("TS", [P, NB])
        IOB = sb("IOB", [P, NB])
        BJ = sb("BJ", [P, VT])
        BJ128 = sb("BJ128", [P, VT])
        TJF = sb("TJF", [P, VT])
        TJ = sb("TJ", [P, VT], I32)
        BT = sb("BT", [VT, P], I32)
        ONES = sb("ONES", [P, P])
        EPSC = sb("EPSC", [P, 1])
        PICK = sb("PICK", [P, 2, CH, P])
        XT = sb("XT", [D + 1, 2, CH * P])
        XG = sb("XG", [P, 2, CH * P])
        R1 = sb("R1", [D + 1, 2, CH * P])
        RZ = sb("RZ", [P, 2, CH, P])
        NN = sb("NN", [P, 2, CH, D])
        DZ = sb("DZ", [P, 2, CH, D])
        TW = sb("TW", [P, 2, CH * TYPES * D])
        WG = sb("WG", [P, 4 * D])
        BG = sb("BG", [1, 2, 4 * D])
        BG3 = sb("BG3", [D + 1, CH * 4 * D], BF16)
        ONE16 = sb("ONE16", [D + 1, P], BF16)
        WT = sb("WT", [D + 1, TYPES * D])
        W01 = sb("W01", [D, D])
        B01 = sb("B01", [D, 1])
        W02 = sb("W02", [D + 1, D])
        W2 = sb("W2", [D, 2, D])
        W3 = sb("W3", [D, 2, D])
        W3A = sb("W3A", [D, D])
        BC = sb("BC", [P, 5, D])
        ST = sb("ST", [P, 8, D])

        Af = A[:, :]
        Hf = H[:, :, :].rearrange("p b f -> p (b f)")
        n3 = VT * 3 * P
        EB = Af[:, 0:n3].bitcast(I32).rearrange("p (g k e) -> p g k e", g=VT, k=3)
        F3 = Af[:, n3:2 * n3].rearrange("p (k g e) -> p k g e", g=VT, k=3)
        SLO = Af[:, 2 * n3:2 * n3 + VT * P].bitcast(I32).rearrange("p (g e) -> p g e", g=VT)
        SHI = OH[:, :, :, :].rearrange("p a u e -> p (a u e)")[:, 0:VT * P].bitcast(I32).rearrange(
            "p (g e) -> p g e", g=VT)
        DSTC = Hf[0:EP, 0:EF].bitcast(I32)
        JUNKV = Hf[0:EP, EF:2 * EF]
        JUNKS = Hf[0:EP, 2 * EF:3 * EF]

        OHf = OH[:, :, :, :].rearrange("p a u e -> p (a u e)")
        DL16 = OHf[:, VT * P:VT * P + VT * P // 2].bitcast(BF16).rearrange("p (g e) -> p g e", g=VT)

        Gf = G[:, :, :, :].rearrange("p h u f -> p (h u f)")
        LOADED = Gf[:, 0:2 * GRP * D].rearrange("p (h u f) -> p h u f", h=2, u=GRP)
        SCALED = Gf[:, 2 * GRP * D:4 * GRP * D].rearrange("p (h u f) -> p h u f", h=2, u=GRP)
        OTS = Hf[:, 0:2 * GRP * P].rearrange("p (h u e) -> p h u e", h=2, u=GRP)
        ACTED = Hf[:, 2 * GRP * P:2 * GRP * (P + D)].rearrange("p (h u f) -> p h u f", h=2, u=GRP)
        AT = Hf[0:1, 2 * GRP * (P + D):2 * GRP * (P + D) + 2 * TRIPS * LPG].bitcast(I32)
        DROW = IDX4[:, 0:GRP * P].bitcast(BF16).rearrange("p (h u e) -> p h u e", h=2, u=GRP)

        M1 = Gf[:, 0:ST_CH * D].rearrange("p (b f) -> p b f", f=D)
        M2 = Gf[:, ST_CH * D:2 * ST_CH * D].rearrange("p (b f) -> p b f", f=D)

        ps_g = ps[:, 0:3072].rearrange("p (h u f) -> p h u f", h=2, f=P)
        ps_t = ps[:, 0:1024].rearrange("p (s f) -> p s f", s=2)
        ps_o = ps[:, 1024:2048].rearrange("p (s f) -> p s f", s=2)
        ps_u = ps[:, 0:2048].rearrange("p (h u f) -> p h u f", h=2, f=D)
        ps_s = ps[:, 2048:4096].rearrange("p (h u f) -> p h u f", h=2, f=D)
        ps_m = ps[:, 2048:3072].rearrange("p (s f) -> p s f", s=2)


        ps_gate = ps_o.rearrange("p s (c f) -> p s c f", c=CH)
        ps_vu = ps_o[:, :, 0:CH * P].rearrange("p s (c f) -> p s c f", c=CH)
        ps_x = ps_o[:, :, 0:CH * D].rearrange("p s (c f) -> p s c f", c=CH)
        tw_v2 = TW[:, :, 0:CH * P].rearrange("p s (c f) -> p s c f", c=CH)

        dst_in, x_in, w_in = sem("dst_in"), sem("x_in"), sem("w_in")
        iota_done = sem("iota_done")
        dve_done = sem("dve_done")
        bounds_set = sem("bounds_set")
        below_v = sem("below_v")
        below_s = sem("below_s")
        totals = sem("totals")
        rows_known = sem("rows_known")
        rows_in = sem("rows_in")
        cols_done = sem("cols_done")
        turned = sem("turned")
        tabled = sem("tabled")
        blk_out, blk_in = sem("blk_out"), sem("blk_in")
        loc_set = sem("loc_set")
        dloc_cast, dloc_out = sem("dloc_cast"), sem("dloc_out")

        centred, squared = sem("centred"), sem("squared")
        varred, rooted = sem("varred"), sem("rooted")
        normed = sem("normed")

        staged = [sem(f"staged{h}") for h in range(2)]
        pool_go = sem("pool_go")
        pe_go = sem("pe_go")
        dve_go = sem("dve_go")
        rows_gated = [sem(f"rows_gated{h}") for h in range(2)]
        rows_other = [sem(f"rows_other{h}") for h in range(2)]
        onehot = [sem(f"onehot{h}") for h in range(2)]
        product = [sem(f"product{h}") for h in range(2)]
        group_added = sem("group_added")
        table_out = sem("table_out")
        chunk_picked = sem("chunk_picked")
        chunk_turned = sem("chunk_turned")
        chunk_copied = sem("chunk_copied")
        chunk_made = sem("chunk_made")
        mlp_in = sem("mlp_in")
        mlp_mid, mlp_act = sem("mlp_mid"), sem("mlp_act")
        mlp_done = sem("mlp_done")
        typ_dve, typ_act = sem("typ_dve"), sem("typ_act")
        typ_out = [sem(f"typ_out{s}") for s in range(2)]
        gru_sig, gru_tanh = sem("gru_sig"), sem("gru_tanh")
        gru_pre, gru_out = sem("gru_pre"), sem("gru_out")
        root_deg, gcn_done, gcn_in = sem("root_deg"), sem("gcn_done"), sem("gcn_in")
        edg_v, edg_sq, edg_u = sem("edg_v"), sem("edg_sq"), sem("edg_u")
        edg_out = [sem(f"edg_out{s}") for s in range(2)]
        kept_out = [sem(f"kept_out{h}") for h in range(2)]
        stat_part, stat_sum, stat_var, stat_root = (sem(f"stat_{n}") for n in ("part", "sum", "var", "root"))
        bn_ready = sem("bn_ready")
        kept_in = [sem(f"kept_in{h}") for h in range(2)]
        drow_in = [sem(f"drow_in{h}") for h in range(2)]
        e_onehot, e_turned, e_picked, e_scaled, e_summed, e_acted, e_product = (
            sem(f"e_{n}") for n in ("onehot", "turned", "picked", "scaled", "summed", "acted", "product"))
        result, stored = sem("result"), sem("stored")

        block = ctx.enter_context(nc.Block())

        def chunks(eng, *parts):
            def turn_of(r, i):
                for lag, part in enumerate(parts):
                    c = r - lag
                    if i is None and 0 <= c < NCH:
                        part(c, c % 2, c // 2)
                    elif i is not None:
                        part(2 * i + c, c % 2, i + c // 2)

            i_first = -(-(1 + len(parts)) // 2)
            for j in range(2 * i_first):
                turn_of(j, None)
            with eng.Fori(i_first, NCH // 2) as i:
                for r in range(2):
                    turn_of(r, i)
            for j in range(2 * (NCH // 2), NCH + len(parts) - 1):
                turn_of(j, None)

        def groups(eng, body):
            for h in range(2):
                body(0, h, True)
            with eng.Fori(1, TRIPS) as i:
                for h in range(2):
                    body(i, h, False)

        def groups_apart(eng, body):
            for h in range(2):
                body(h, h, 0)
            with eng.Fori(1, TRIPS) as i:
                for h in range(2):
                    body(2 * i + h, h, i)

        def static(v, least=1):
            return not isinstance(v, int) or v >= least

        def group_cols(t, i, h):
            return t[:, bass.ds(i * (2 * GRP) + h * GRP, GRP)]

        def two(t, c):
            return t[:, bass.ds(c * CH, CH), :]

        def table_rows(t, r):
            return t.rearrange("(p c r) f -> p c (r f)", p=P, c=NCH)

        @block.sync
        def _(sp):
            sp.dma_start(DSTC, dst.rearrange("(p f) -> p f", p=EP)).then_inc(dst_in, 16)
            sp.dma_start(X[:, :, :], x).then_inc(x_in, 16)
            loads = [(W01[:, :], L0_W1), (B01[:, :], L0_b1.rearrange("(p a) -> p a", a=1)),
                     (W02[0:D, :], L0_W2), (W02[D:D + 1, :], L0_b2.rearrange("(a n) -> a n", a=1)),
                     (WT[0:D, :], L1_Wt), (WT[D:D + 1, :], L1_b),
                     (WG[0:D, 0:3 * D], L1_wih), (WG[D:P, 0:2 * D], L1_whh[:, 0:2 * D]),
                     (WG[D:P, 3 * D:4 * D], L1_whh[:, 2 * D:3 * D]),
                     (BG[:, 0, 0:3 * D], L1_bih), (BG[:, 1, 0:2 * D], L1_bhh[:, 0:2 * D]),
                     (BG[:, 1, 3 * D:4 * D], L1_bhh[:, 2 * D:3 * D]),
                     (W2[:, 0, :], L2_W1), (W2[:, 1, :], L2_W2),
                     (W3A[:, :], L3_Wt[0:D, :]), (W3[:, 0, :], L3_Wt[D:P, :])]
            loads += [(BC[:, k, :], r.partition_broadcast(P)) for k, r in
                      enumerate((L2_b1, L2_b2, L3_b, L3_gamma, L3_beta))]
            assert len(loads) == LOADS
            for o, i in loads:
                sp.dma_start(o, i).then_inc(w_in, 16)

            sp.wait_ge(dloc_cast, 1)
            sp.dma_start(dloc_dram.rearrange("(g p) e -> p g e", p=P), DL16).then_inc(dloc_out, 16)

            sp.wait_ge(tabled, 4)
            sp.dma_start(blk_dram, BT[:, :]).then_inc(blk_out, 16)
            sp.wait_ge(blk_out, 16)
            sp.dma_start(BLK[:, :], blk_dram.rearrange("g (a e) -> a (g e)", a=1)).then_inc(blk_in, 16)

            sp.wait_ge(normed, 1)
            sp.dma_start(tab_gin.rearrange("(p b) f -> p b f", p=P), H[:, :, :]).then_inc(table_out, 16)

            gated = table_rows(tab_gated, CH * TYPES)
            with sp.Fori(0, STEPS) as step:
                def send(c, s, i):
                    sp.wait_ge(typ_dve, step * NCH + c + 1)
                    sp.wait_ge(typ_act, step * NCH + c + 1)
                    sp.dma_start(gated[:, bass.ds(c, 1), :], TW[:, s:s + 1, :]).then_inc(typ_out[s], 16)
                chunks(sp, send)

            for k in range(2):
                sp.wait_ge(gcn_done, (k + 1) * NCH)
                sp.dma_start(tab_gcn[k].rearrange("(p b) f -> p b f", p=P), FEAT).then_inc(table_out, 16)

            edge = table_rows(tab_edge, CH)

            def send_edge(c, s, i):
                sp.wait_ge(edg_v, c + 1)
                sp.wait_ge(edg_sq, c + 1)
                sp.dma_start(edge[:, bass.ds(c, 1), :], TW[:, s:s + 1, 0:CH * 2 * D]).then_inc(edg_out[s], 16)
            chunks(sp, send_edge)

            def keep(i, h, first):
                sp.wait_ge(rows_other[h], 16 * GRP * (3 * TRIPS + i + 1))
                sp.dma_start(kept[:, bass.ds(i * (2 * GRP) + h * GRP, GRP), :],
                             G[:, h, :, 0:D]).then_inc(kept_out[h], 16)
            groups(sp, keep)
            for h in range(2):
                sp.wait_ge(kept_out[h], TRIPS * 16)

            sp.wait_ge(bn_ready, 1)

            def load_kept(g, h, i):
                if static(g, 2):
                    sp.wait_ge(e_scaled, g - 1)
                sp.dma_start(LOADED[:, h, :, :], kept[:, bass.ds(g * GRP, GRP), :]).then_inc(kept_in[h], 16)
                if static(g, 2):
                    sp.wait_ge(e_turned, g - 1)
                sp.dma_start(DROW[:, h, :, :].rearrange("p u e -> p (u e)"),
                             dloc_dram[bass.ds(g * GRP, GRP), :].rearrange("u e -> (u e)").partition_broadcast(P)
                             ).then_inc(drow_in[h], 16)
            groups_apart(sp, load_kept)
            sp.wait_ge(result, 1)
            sp.dma_start(out, X[:, :, :]).then_inc(stored, 16)
            sp.wait_ge(stored, 16)

        @block.gpsimd
        def _(pool):
            kw = dict(allow_small_or_imprecise_dtypes=True)
            nc.gpsimd.iota(IOTAR[:, :], [[1, P]], base=0, channel_multiplier=0, **kw).then_inc(iota_done, 1)
            nc.gpsimd.iota(VIS[:, :], [[P, VT]], base=0, channel_multiplier=1, **kw).then_inc(iota_done, 1)
            nc.gpsimd.iota(BND[:, :], [[P, NB]], base=P, channel_multiplier=0, **kw).then_inc(iota_done, 1)
            nc.gpsimd.iota(IOB[:, :], [[1, NB]], base=1, channel_multiplier=0, **kw).then_inc(iota_done, 1)
            pool.wait_ge(rows_known, 1)
            for g in range(VT):
                nc.gpsimd.indirect_dma_start(
                    out=EB[:, g, :, :].rearrange("p k e -> p (k e)"), out_offset=None, in_=edges,
                    in_offset=bass.IndirectOffsetOnAxis(ap=TJ[:, g:g + 1], axis=0)).then_inc(rows_in, 16)

            def gather(n, table, width, rows):
                def body(i, h, first):
                    pool.wait_ge(staged[h], n * TRIPS + i + 1)
                    pool.sem_inc(pool_go, 1)
                    if width == 2 * D and not first:
                        pool.wait_ge(kept_out[h], i * 16)
                        pool.sem_inc(pool_go, 1)
                    for u in range(GRP):
                        nc.gpsimd.indirect_dma_start(
                            out=G[:, h, u, 0:width], out_offset=None, in_=table,
                            in_offset=bass.IndirectOffsetOnAxis(ap=STG[:, h, u:u + 1], axis=0)
                        ).then_inc(rows[h], 16)
                groups(pool, body)

            def pick(run, src, width):
                def body(c, s, i):
                    if static(i):
                        pool.wait_ge(chunk_turned, run * NCH + c - 1)
                        pool.sem_inc(pool_go, 1)
                    nc.gpsimd.tensor_copy(PICK[:, s, :, 0:width], two(src, c)).then_inc(chunk_picked, 1)
                chunks(pool, body)

            pool.wait_ge(table_out, 16)
            gather(0, tab_gin, D, rows_other)
            pool.wait_ge(mlp_in, 1)
            pick(RUN_MLP, H, D)
            with pool.Fori(0, STEPS) as step:
                pool.wait_ge(group_added, (step + 1) * GK + 1)
                pool.sem_inc(pool_go, 1)
                pick(2 * step + RUN_TYPE, FEAT, D)
                for s in range(2):
                    pool.wait_ge(typ_out[s], (step + 1) * SLOT_DMAS[s])
                    pool.sem_inc(pool_go, 1)
                gather(step + 1, tab_gated, D, rows_gated)
                pool.wait_ge(group_added, (step + 2) * GK)
                pool.sem_inc(pool_go, 1)
                pick(2 * step + RUN_GRU, A3, P)
            for k in range(2):
                pool.wait_ge(gcn_in, k + 1)
                pick(RUN_GCN + k, H, D)
                pool.wait_ge(table_out, 16 * (k + 2))
                gather(STEPS + 1 + k, tab_gcn[k], D, rows_other)
            pool.wait_ge(normed, 4)
            pick(RUN_EDGE, H, D)
            for s in range(2):
                pool.wait_ge(edg_out[s], SLOT_DMAS[s])
            gather(LAST_PASS, tab_edge, 2 * D, rows_other)

            scale = ST[:, S_SCALE:S_SCALE + 1, :].broadcast_to([P, GRP, D])
            pool.wait_ge(bn_ready, 1)

            def scale_rows(g, h, i):
                pool.wait_ge(kept_in[h], i * 16 + 16)
                pool.sem_inc(pool_go, 1)
                if static(g, 2):
                    pool.wait_ge(e_acted, g - 1)
                    pool.sem_inc(pool_go, 1)
                nc.gpsimd.tensor_tensor(SCALED[:, h, :, :], LOADED[:, h, :, :], scale, ALU.mult).then_inc(e_scaled, 1)
            groups_apart(pool, scale_rows)

        @block.scalar
        def _(act):
            act.wait_ge(dst_in, 16)
            act.wait_ge(bounds_set, 1)
            with act.Fori(0, NB // 2) as k:
                nc.scalar.activation(JUNKS, DSTC, ACT.Sign, bias=BNDH[0:EP, bass.ds(2 * k + 1, 1)], scale=-1.0,
                                     accum_out=CNTB[0:EP, bass.ds(2 * k + 1, 1)]).then_inc(below_s, 1)
                act.wait_ge(below_s, k + 1)

            act.wait_ge(cols_done, 1)
            nc.scalar.copy(DL16, F3[:, 0, :, :]).then_inc(dloc_cast, 1)

            for k, table in enumerate((DLOC, IDX, IDX4)):
                act.wait_ge(turned, k + 1)
                half = 2048 * (k % 2)
                nc.scalar.copy(table[:, :], ps[:, half:half + VT * P]).then_inc(tabled, 1)
            act.wait_ge(turned, 4)
            nc.scalar.copy(BT[:, :], ps[0:VT, 2048:2048 + P]).then_inc(tabled, 1)

            def norm(n):
                act.wait_ge(centred, n + 1)
                nc.scalar.activation(SUMS, H[:, :, :], ACT.Square).then_inc(squared, 1)
                act.wait_ge(varred, n + 1)
                nc.scalar.activation(SB[:, :], SA[:, :], ACT.Sqrt, bias=EPSC[:, 0:1], scale=1.0 / D
                                     ).then_inc(rooted, 1)

            def stage_indices(n, table):
                def body(i, h, first):
                    if not first:
                        act.wait_ge(product[h], n * TRIPS + i)
                    nc.scalar.copy(STG[:, h, :], group_cols(table, i, h)).then_inc(staged[h], 1)
                groups(act, body)

            norm(0)
            act.wait_ge(tabled, 4)
            stage_indices(0, IDX)

            def copied(run, dst, rows):
                def part(c, s, i):
                    act.wait_ge(chunk_turned, run * NCH + c + 1)
                    nc.scalar.copy(dst[0:rows, s, :], ps_t[0:rows, s, 0:CH * P]).then_inc(chunk_copied, 1)
                return part

            def mlp_relu(c, s, i):
                act.wait_ge(mlp_mid, c + 1)
                nc.scalar.activation(R1[0:D, s, :], ps_m[0:D, s, 0:CH * P], ACT.Relu, bias=B01[:, 0:1]
                                     ).then_inc(mlp_act, 1)
            chunks(act, copied(RUN_MLP, XT, D), mlp_relu)

            norm(1)

            with act.Fori(0, STEPS) as step:
                def type_chunk(c, s, i):
                    act.wait_ge(chunk_made, (2 * step + RUN_TYPE) * NCH + c + 1)
                    if static(i):
                        act.wait_ge(typ_out[s], step * SLOT_DMAS[s] + i * 16)
                    nc.scalar.copy(TW[:, s, 0:TYPES * D], ps_o[:, s, 0:TYPES * D]).then_inc(typ_act, 1)
                chunks(act, copied(2 * step + RUN_TYPE, XT, D), type_chunk)
                stage_indices(step + 1, IDX4)

                def gru_sigmoid(c, s, i):
                    act.wait_ge(chunk_made, (2 * step + RUN_GRU) * NCH + c + 1)
                    if static(i):
                        act.wait_ge(gru_out, step * (NCH * 3) + (c - 1) * 3)
                    nc.scalar.activation(RZ[:, s, :, :], ps_gate[:, s, :, 0:2 * D], ACT.Sigmoid).then_inc(gru_sig, 1)

                def gru_tanh_n(c, s, i):
                    act.wait_ge(gru_pre, step * (NCH * 2) + c * 2 + 2)
                    nc.scalar.activation(NN[:, s, :, :], NN[:, s, :, :], ACT.Tanh).then_inc(gru_tanh, 1)
                chunks(act, copied(2 * step + RUN_GRU, XG, P), gru_sigmoid, gru_tanh_n)

            act.wait_ge(normed, 2)
            nc.scalar.activation(SC[:, :], CNT[:, :], ACT.Sqrt, bias=ONES[:, 0:1]).then_inc(root_deg, 1)
            norm(2)
            for k in range(2):
                chunks(act, copied(RUN_GCN + k, XT, D))
                stage_indices(STEPS + 1 + k, IDX)

            norm(3)

            def edge_chunk(c, s, i):
                act.wait_ge(edg_v, c + 1)
                nc.scalar.activation(tw_v2[:, s, :, D:P], tw_v2[:, s, :, 0:D], ACT.Square).then_inc(edg_sq, 1)
            chunks(act, copied(RUN_EDGE, XT, D), edge_chunk)
            stage_indices(LAST_PASS, IDX)

            act.wait_ge(stat_var, 1)
            nc.scalar.activation(ST[:, S_ROOT, :], ST[:, S_VAR, :], ACT.Sqrt, bias=EPSC[:, 0:1]).then_inc(stat_root, 1)

        @block.tensor
        def _(pe):
            pe.wait_ge(below_v, NB // 2)
            pe.wait_ge(below_s, NB // 2)
            nc.tensor.matmul(ps[:, 0:NB], ONES[0:EP, :], CNTB[0:EP, :], start=True, stop=True).then_inc(totals, 1)

            pe.wait_ge(cols_done, 1)
            for k in range(3):
                if k == 2:
                    pe.wait_ge(tabled, 1)
                half = 2048 * (k % 2)
                for g in range(VT):
                    ins = nc.tensor.transpose(ps[:, half + g * P:half + (g + 1) * P], F3[:, k, g, :], IDENT[:, :])
                ins.then_inc(turned, 1)
            pe.wait_ge(tabled, 2)
            nc.tensor.transpose(ps[0:VT, 2048:2048 + P], BJ128[:, :], IDENT[:, :]).then_inc(turned, 1)

            def load_places(table, g, most):
                places = []
                for q in range(QUADS):
                    _, regs = nc.values_load_multi_w_load_instructions(
                        table[0:1, bass.ds(g * LPG + 4 * q, 4)], engines=[mybir.EngineType.PE], min_val=0,
                        max_val=most, skip_runtime_bounds_check_because="at most ten blocks in a group")
                    places += list(regs)
                return places[:GRP]

            def zero(base, columns):
                for b in range(0, columns, 512):
                    w = min(512, columns - b)
                    nc.tensor.matmul(ps[:, base + b:base + b + w], ZERO[:, 0:P], ZERO[:, 0:w], start=True, stop=True)

            def accumulate(base, place, width, onehots_, rows_):
                return nc.tensor.matmul(ps[:, base:][:, bass.ds(place, width)], onehots_, rows_, start=False,
                                        stop=False, skip_group_check=True)

            def products(n, width, rows, m):
                def body(i, h, first):
                    base = h * 1536
                    places = load_places(LOC, 2 * i + h, (GRP - 1) * P)
                    if not first:
                        pe.wait_ge(group_added, n * GK + 2 * i + h)
                        pe.sem_inc(pe_go, 1)
                    zero(base, GRP * P)
                    pe.wait_ge(onehot[h], n * TRIPS + i + 1)
                    pe.wait_ge(rows[h], (m * TRIPS + i + 1) * (16 * GRP))
                    for u in range(GRP):
                        ins = accumulate(base, places[u], width, OH[:, h, u, :], G[:, h, u, 0:width])
                    ins.then_inc(product[h], 1)
                groups(pe, body)

            def turn(run, width):
                def part(c, s, i):
                    pe.wait_ge(chunk_picked, run * NCH + c + 1)
                    pe.sem_inc(pe_go, 1)
                    for k in range(CH):
                        ins = nc.tensor.transpose(ps_t[0:width, s, k * P:(k + 1) * P], PICK[:, s, k, 0:width],
                                                  IDENT[:, :])
                    ins.then_inc(chunk_turned, 1)
                return part

            pe.wait_ge(tabled, 4)
            pe.wait_ge(loc_set, 1)
            products(0, D + 1, rows_other, 0)

            pe.wait_ge(w_in, 16 * LOADS)
            pe.wait_ge(mlp_in, 1)

            def mlp_hidden(c, s, i):
                pe.wait_ge(chunk_copied, RUN_MLP * NCH + c + 1)
                pe.sem_inc(pe_go, 1)
                nc.tensor.matmul(ps_m[0:D, s, 0:CH * P], W01[:, :], XT[0:D, s, :], start=True, stop=True
                                 ).then_inc(mlp_mid, 1)

            def mlp_out(c, s, i):
                pe.wait_ge(mlp_act, c + 1)
                if static(i):
                    pe.wait_ge(mlp_done, c - 1)
                for k in range(CH):
                    ins = nc.tensor.matmul(ps_x[:, s, k, :], R1[:, s, k * P:(k + 1) * P], W02[:, :],
                                           start=True, stop=True)
                ins.then_inc(chunk_made, 1)
            chunks(pe, turn(RUN_MLP, D), mlp_hidden, mlp_out)

            with pe.Fori(0, STEPS) as step:
                def type_chunk(c, s, i):
                    pe.wait_ge(chunk_copied, (2 * step + RUN_TYPE) * NCH + c + 1)
                    if static(i):
                        pe.wait_ge(typ_dve, step * NCH + c - 1)
                        pe.wait_ge(typ_act, step * NCH + c - 1)
                    for k, bank in enumerate((ps_o, ps_m)):
                        ins = nc.tensor.matmul(bank[:, s, 0:TYPES * D], XT[:, s, k * P:(k + 1) * P], WT[:, :],
                                               start=True, stop=True)
                    ins.then_inc(chunk_made, 1)
                chunks(pe, turn(2 * step + RUN_TYPE, D), type_chunk)
                pe.wait_ge(typ_dve, (step + 1) * NCH)
                pe.wait_ge(typ_act, (step + 1) * NCH)
                pe.sem_inc(pe_go, 1)
                products(step + 1, D, rows_gated, step)

                pe.wait_ge(group_added, (step + 2) * GK)

                def gru_chunk(c, s, i):
                    pe.wait_ge(chunk_copied, (2 * step + RUN_GRU) * NCH + c + 1)
                    if static(i):
                        pe.wait_ge(gru_pre, step * (NCH * 2) + (c - 1) * 2)
                    nc.tensor.matmul(ps_o[:, s, :], ONE16[:, :], BG3[:, :], start=True, stop=True)
                    for k in range(CH):
                        ins = nc.tensor.matmul(ps_gate[:, s, k, :], XG[:, s, k * P:(k + 1) * P], WG[:, :],
                                               start=False, stop=False, skip_group_check=True)
                    ins.then_inc(chunk_made, 1)
                chunks(pe, turn(2 * step + RUN_GRU, P), gru_chunk)
                pe.wait_ge(gru_pre, (step + 1) * (NCH * 2))

            for n in range(2):
                def gcn_chunk(c, s, i):
                    pe.wait_ge(chunk_copied, (RUN_GCN + n) * NCH + c + 1)
                    if static(i):
                        pe.wait_ge(gcn_done, n * NCH + c - 1)
                    for k in range(CH):
                        ins = nc.tensor.matmul(ps_x[:, s, k, :], XT[0:D, s, k * P:(k + 1) * P], W2[:, n, :],
                                               start=True, stop=True)
                    ins.then_inc(chunk_made, 1)
                chunks(pe, turn(RUN_GCN + n, D), gcn_chunk)
                pe.wait_ge(gcn_done, (n + 1) * NCH)
                products(STEPS + 1 + n, D, rows_other, 1 + n)
                pe.wait_ge(group_added, (STEPS + 2 + n) * GK)

            def edge_chunk(c, s, i):
                pe.wait_ge(chunk_copied, RUN_EDGE * NCH + c + 1)
                if static(i):
                    pe.wait_ge(edg_u, c - 1)
                for k in range(CH):
                    ins = nc.tensor.matmul(ps_vu[:, s, k, :], XT[0:D, s, k * P:(k + 1) * P],
                                           W3[:, :, :].rearrange("p a f -> p (a f)"), start=True, stop=True)
                ins.then_inc(chunk_made, 1)
            chunks(pe, turn(RUN_EDGE, D), edge_chunk)
            pe.wait_ge(edg_u, NCH)
            products(LAST_PASS, 2 * D, rows_other, 3)

            pe.wait_ge(stat_part, 1)
            nc.tensor.matmul(ps[:, 0:2 * D], ONES[:, :], ST[:, S_SUM:S_SQ + 1, :].rearrange("p a f -> p (a f)"),
                             start=True, stop=True).then_inc(stat_sum, 1)

            pe.wait_ge(bn_ready, 1)

            def pick_u(g, h):
                at = load_places(AT, g, (NB - 1) * P)
                if static(g, 2):
                    pe.wait_ge(e_summed, g - 1)
                pe.wait_ge(e_turned, g + 1)
                for u in range(GRP):
                    ins = nc.tensor.matmul(ps_u[:, h, u, :], OTS[:, h, u, :], A[:, D:][:, bass.ds(at[u], D)],
                                           start=True, stop=True)
                ins.then_inc(e_picked, 1)

            def sum_group(g, h, i):
                if not isinstance(g, int) or g < 2 * TRIPS - 1:
                    pick_u(g + 1, 1 - h)
                base = 2048 + 1024 * h
                places = load_places(LOC, g, (GRP - 1) * D)
                if static(g, 2):
                    pe.wait_ge(group_added, (LAST_PASS + 1) * GK + g)
                    pe.sem_inc(pe_go, 1)
                zero(base, GRP * D)
                pe.wait_ge(e_onehot, g + 1)
                pe.wait_ge(e_acted, g + 1)
                for u in range(GRP):
                    ins = accumulate(base, places[u], D, OH[:, h, u, :], ACTED[:, h, u, :])
                ins.then_inc(e_product, 1)
            pick_u(0, 0)
            sum_group(0, 0, 0)
            with pe.Fori(0, TRIPS - 1) as i:
                sum_group(2 * i + 1, 1, i)
                sum_group(2 * i + 2, 0, i)
            sum_group(2 * TRIPS - 1, 1, 0)

        @block.vector
        def _(dve):
            count = [0]

            def link(ins):
                count[0] += 1
                ins.then_inc(dve_done, 1)
                dve.wait_ge(dve_done, count[0])

            V = nc.vector

            V.memset(EPSC[:, :], EPS)
            V.memset(ZERO[:, :], 0.0)
            V.memset(ONE16[:, :], 1.0)
            V.memset(BG3[:, :], 0.0)
            V.memset(LOC[:, :], 0)
            V.memset(ONES[:, :], 1.0)
            V.memset(XT[D:D + 1, :, :], 1.0)
            V.memset(R1[D:D + 1, :, :], 1.0)
            V.memset(CNTB[:, :], 0.0)
            V.memset(WG[0:D, 3 * D:4 * D], 0.0)
            V.memset(WG[D:P, 2 * D:3 * D], 0.0)
            V.memset(BG[:, 0, 3 * D:4 * D], 0.0)
            V.memset(BG[:, 1, 2 * D:3 * D], 0.0)
            dve.wait_ge(iota_done, 4)
            V.tensor_scalar(IDENT[:, :], IOTAR[:, :], VIS[:, 0:1], None, ALU.is_equal)
            V.tensor_scalar(BNDH[:, :], BND[:, :], -0.5, None, ALU.add).then_inc(bounds_set, 1)

            dve.wait_ge(bounds_set, 1)
            dve.wait_ge(dst_in, 16)
            with dve.Fori(0, NB // 2) as k:
                V.tensor_scalar(JUNKV, DSTC, BND[0:EP, bass.ds(2 * k, 1)], 0.0, ALU.is_lt, ALU.add,
                                accum_out=CNTB[0:EP, bass.ds(2 * k, 1)]).then_inc(below_v, 1)
                dve.wait_ge(below_v, k + 1)

            dve.wait_ge(totals, 1)
            even = ps[:, 0:NB].rearrange("p (b two) -> p two b", two=2)
            to = TOT[:, :].rearrange("p (b two) -> p two b", two=2)
            link(V.tensor_copy(to[:, 0, :], even[:, 0, :]))
            link(V.tensor_scalar(to[:, 1, :], even[:, 1, :], 0.5, E / 2.0, ALU.mult, ALU.add))
            link(V.tensor_scalar(TOT[:, :], TOT[:, :], 7, None, ALU.arith_shift_right))
            link(V.tensor_tensor(TS[:, :], TOT[:, :], IOB[:, :], ALU.add))
            for g in range(VT):
                link(V.tensor_scalar(CNTB[:, 0:NB - 1], TS[:, 0:NB - 1], VIS[:, g:g + 1], 0.0, ALU.is_le, ALU.add,
                                     accum_out=BJ[:, g:g + 1]))
            link(V.tensor_tensor(TJF[:, :], VIS[:, :], BJ[:, :], ALU.subtract))
            V.tensor_scalar(TJ[:, :], TJF[:, :], float(ROWS - 1), None, ALU.min).then_inc(rows_known, 1)
            link(V.tensor_scalar(BJ128[:, :], BJ[:, :], float(P), None, ALU.mult))

            dve.wait_ge(rows_in, 16 * VT)
            for g in range(VT):
                V.tensor_scalar(F3[:, 0, g, :], EB[:, g, 0, :], BJ128[:, g:g + 1], None, ALU.subtract)
            V.tensor_scalar(SLO, EB[:, :, 1, :], P - 1, None, ALU.bitwise_and)
            link(V.tensor_scalar(SHI, EB[:, :, 1, :], 7, None, ALU.arith_shift_right))
            link(V.scalar_tensor_tensor(F3[:, 1, :, :], SLO, float(NB), SHI, ALU.mult, ALU.add))
            V.scalar_tensor_tensor(F3[:, 2, :, :], F3[:, 1, :, :], float(TYPES), EB[:, :, 2, :], ALU.mult, ALU.add
                                   ).then_inc(cols_done, 1)

            def over_f(t):
                return t[:, :].unsqueeze(2).broadcast_to([P, NB, D])

            def over_b(k):
                return BC[:, k:k + 1, :].broadcast_to([P, NB, D])

            def norm(n, to):
                link(V.tensor_reduce(SA[:, :], X[:, :, :], AX_X, ALU.add))
                link(V.tensor_scalar(SA[:, :], SA[:, :], -1.0 / D, None, ALU.mult))
                V.tensor_tensor(H[:, :, :], X[:, :, :], over_f(SA), ALU.add).then_inc(centred, 1)
                dve.wait_ge(squared, n + 1)
                V.tensor_reduce(SA[:, :], SUMS, AX_X, ALU.add).then_inc(varred, 1)
                dve.wait_ge(rooted, n + 1)
                link(V.reciprocal(SB[:, :], SB[:, :]))
                V.scalar_tensor_tensor(to, H[:, :, :], 0.0, over_f(SB), ALU.max, ALU.mult).then_inc(normed, 1)

            def clear(view):
                V.memset(view, 0.0).then_inc(group_added, 1)

            def add_group(n, g, products_, width):
                b = dve.value_load(FIRST[0:1, bass.ds(g, 1)], min_val=0, max_val=NB - GRP)
                sums = A3[:, bass.ds(b, GRP), 0:width]
                dve.wait_ge(group_added, n * GK + g + 1)
                return V.tensor_tensor(sums, sums, products_[:, 0:GRP, 0:width], ALU.add).then_inc(group_added, 1)

            def onehots(cols, h):
                return V.tensor_tensor(OH[:, h, :, :], IOTAR[:, :].unsqueeze(1).broadcast_to([P, GRP, P]),
                                       cols.unsqueeze(2).broadcast_to([P, GRP, P]), ALU.is_equal)

            def sum_edges(n, width):
                for h in range(2):
                    onehots(group_cols(DLOC, 0, h), h).then_inc(onehot[h], 1)

                def add(i, h):
                    dve.wait_ge(product[h], n * TRIPS + i + 1)
                    dve.sem_inc(dve_go, 1)
                    add_group(n, 2 * i + h, ps_g[:, h, :, :], width)
                with dve.Fori(0, TRIPS - 1) as i:
                    for h in range(2):
                        add(i, h)
                        onehots(group_cols(DLOC, i + 1, h), h).then_inc(onehot[h], 1)
                for h in range(2):
                    add(TRIPS - 1, h)
                dve.wait_ge(group_added, (n + 1) * GK)

            dve.wait_ge(x_in, 16)
            norm(0, H[:, :, :])
            V.memset(G[:, :, :, D:D + 1], 1.0)
            clear(A3[:, :, 0:D + 1])
            dve.wait_ge(tabled, 4)
            dve.wait_ge(blk_in, 16)
            blk = BLK[:, 0:VISITS].rearrange("a (g u) -> a g u", u=GRP)
            loc = LOC[:, :].rearrange("a (g u) -> a g u", u=LPG)[:, :, 0:GRP]
            first = FIRST[:, :].unsqueeze(2)
            link(V.tensor_scalar(first, blk[:, :, 0:1], (NB - GRP) * P, None, ALU.min))
            link(V.tensor_tensor(loc, blk, first.broadcast_to([1, 2 * TRIPS, GRP]), ALU.subtract))
            link(V.tensor_scalar(FIRST[:, :], FIRST[:, :], 7, None, ALU.arith_shift_right))
            dve.sem_inc(loc_set, 1)
            dve.wait_ge(dloc_out, 16)
            sum_edges(0, D + 1)
            V.tensor_copy(CNT[:, :].unsqueeze(2), A3[:, :, D:D + 1])
            dve.wait_ge(table_out, 16)
            V.tensor_tensor(H[:, :, :], H[:, :, :], SUMS, ALU.add).then_inc(mlp_in, 1)

            def mlp_chunk(c, s, i):
                dve.wait_ge(chunk_made, RUN_MLP * NCH + c + 1)
                V.scalar_tensor_tensor(two(X, c), ps_x[:, s, :, :], 0.0, two(X, c), ALU.max, ALU.add
                                       ).then_inc(mlp_done, 1)
            chunks(dve, mlp_chunk)
            dve.wait_ge(mlp_done, NCH)

            total, rest = BG[:, 0, :], BG[:, 1, :]
            link(V.tensor_tensor(total, total, rest, ALU.add))
            for part in range(3):
                one = BG3[32 * part:32 * part + 1, :].rearrange("a (k f) -> a k f", k=CH)
                link(V.tensor_copy(one, total.unsqueeze(1).broadcast_to([1, CH, 4 * D])))
                if part < 2:
                    link(V.tensor_copy(rest, one[:, 0, :]))
                    link(V.tensor_tensor(total, total, rest, ALU.subtract))
            norm(1, FEAT)
            with dve.Fori(0, STEPS) as step:
                clear(SUMS)

                def type_chunk(c, s, i):
                    dve.wait_ge(chunk_made, (2 * step + RUN_TYPE) * NCH + c + 1)
                    if static(i):
                        dve.wait_ge(typ_out[s], step * SLOT_DMAS[s] + i * 16)
                    V.tensor_copy(TW[:, s, TYPES * D:], ps_m[:, s, 0:TYPES * D]).then_inc(typ_dve, 1)
                chunks(dve, type_chunk)
                sum_edges(step + 1, D)

                def gru_new(c, s, i):
                    done = step * (NCH * 2) + c * 2
                    dve.wait_ge(gru_sig, step * NCH + c + 1)
                    V.tensor_tensor(NN[:, s, :, :], RZ[:, s, :, 0:D], ps_gate[:, s, :, 3 * D:4 * D], ALU.mult
                                    ).then_inc(gru_pre, 1)
                    dve.wait_ge(gru_pre, done + 1)
                    V.tensor_tensor(NN[:, s, :, :], NN[:, s, :, :], ps_gate[:, s, :, 2 * D:3 * D], ALU.add
                                    ).then_inc(gru_pre, 1)

                def gru_mix(c, s, i):
                    done = step * (NCH * 3) + c * 3
                    feat, z = two(FEAT, c), RZ[:, s, :, D:2 * D]
                    dve.wait_ge(gru_tanh, step * NCH + c + 1)
                    V.tensor_tensor(DZ[:, s, :, :], feat, NN[:, s, :, :], ALU.subtract).then_inc(gru_out, 1)
                    dve.wait_ge(gru_out, done + 1)
                    V.tensor_tensor(DZ[:, s, :, :], DZ[:, s, :, :], z, ALU.mult).then_inc(gru_out, 1)
                    dve.wait_ge(gru_out, done + 2)
                    V.tensor_tensor(feat, NN[:, s, :, :], DZ[:, s, :, :], ALU.add).then_inc(gru_out, 1)
                chunks(dve, gru_new, gru_mix)
                dve.wait_ge(gru_out, (step + 1) * (NCH * 3))
            link(V.tensor_tensor(X[:, :, :], X[:, :, :], FEAT, ALU.add))

            norm(2, H[:, :, :])
            dve.wait_ge(root_deg, 1)
            link(V.reciprocal(DINV[:, :], SC[:, :]))
            for k in range(2):
                clear(SUMS)
                dve.wait_ge(group_added, (STEPS + 1 + k) * GK + 1)
                dve.sem_inc(gcn_in, 1)

                def gcn_chunk(c, s, i):
                    dve.wait_ge(chunk_made, (RUN_GCN + k) * NCH + c + 1)
                    scale = DINV[:, bass.ds(c * CH, CH)].unsqueeze(2).broadcast_to([P, CH, D])
                    V.tensor_tensor(two(FEAT, c), ps_x[:, s, :, :], scale, ALU.mult).then_inc(gcn_done, 1)
                chunks(dve, gcn_chunk)
                sum_edges(STEPS + 1 + k, D)
                link(V.tensor_tensor(H[:, :, :], SUMS, FEAT, ALU.add))
                link(V.tensor_tensor(H[:, :, :], H[:, :, :], over_f(DINV), ALU.mult))
                link(V.tensor_tensor(H[:, :, :], H[:, :, :], over_b(k), ALU.add))
                if k == 0:
                    link(V.tensor_scalar(H[:, :, :], H[:, :, :], 0.0, None, ALU.max))
                    dve.wait_ge(table_out, 32)
                else:
                    link(V.tensor_tensor(X[:, :, :], X[:, :, :], H[:, :, :], ALU.add))

            link(V.tensor_tensor(W3[:, 1, :], W3A[:, :], W3[:, 0, :], ALU.subtract))
            norm(3, H[:, :, :])
            clear(A3)

            def edge_chunk(c, s, i):
                dve.wait_ge(chunk_made, RUN_EDGE * NCH + c + 1)
                if static(i):
                    dve.wait_ge(edg_out[s], i * 16)
                V.tensor_copy(tw_v2[:, s, :, 0:D], ps_vu[:, s, :, 0:D]).then_inc(edg_v, 1)
                V.tensor_copy(two(H, c), ps_vu[:, s, :, D:P]).then_inc(edg_u, 1)
            chunks(dve, edge_chunk)
            sum_edges(LAST_PASS, 2 * D)

            link(V.memset(ST[:, S_SUM:S_SQ + 1, :], 0.0))
            for h in range(2):
                dve.wait_ge(kept_out[h], TRIPS * 16)
            for j in range(0, NB, ST_CH):
                u, s1, s2 = H[:, j:j + ST_CH, :], SUMS[:, j:j + ST_CH, :], FEAT[:, j:j + ST_CH, :]
                deg = CNT[:, j:j + ST_CH].unsqueeze(2).broadcast_to([P, ST_CH, D])
                link(V.tensor_tensor(M1, u, deg, ALU.mult))
                link(V.scalar_tensor_tensor(M2, s1, 2.0, M1, ALU.mult, ALU.add))
                link(V.tensor_tensor(M2, M2, u, ALU.mult))
                link(V.tensor_tensor(M2, M2, s2, ALU.add))
                link(V.tensor_tensor(M1, M1, s1, ALU.add))
                for m, row in ((M1, S_SUM), (M2, S_SQ)):
                    link(V.tensor_reduce(ST[:, S_TMP, :], m.rearrange("p b f -> p f b"), AX_X, ALU.add))
                    link(V.tensor_tensor(ST[:, row, :], ST[:, row, :], ST[:, S_TMP, :], ALU.add))
            dve.sem_inc(stat_part, 1)

            bias, gamma, beta = (BC[:, k, :] for k in (2, 3, 4))
            dve.wait_ge(stat_sum, 1)
            link(V.tensor_scalar(ST[:, S_MEAN, :], ps[:, 0:D], 1.0 / E, None, ALU.mult))
            link(V.tensor_scalar(ST[:, S_VAR, :], ps[:, D:2 * D], 1.0 / E, None, ALU.mult))
            link(V.tensor_tensor(ST[:, S_TMP, :], ST[:, S_MEAN, :], ST[:, S_MEAN, :], ALU.mult))
            link(V.tensor_tensor(ST[:, S_VAR, :], ST[:, S_VAR, :], ST[:, S_TMP, :], ALU.subtract))
            V.tensor_scalar(ST[:, S_VAR, :], ST[:, S_VAR, :], 0.0, None, ALU.max).then_inc(stat_var, 1)
            link(V.tensor_tensor(ST[:, S_MEAN, :], ST[:, S_MEAN, :], bias, ALU.add))
            dve.wait_ge(stat_root, 1)
            link(V.reciprocal(ST[:, S_SCALE, :], ST[:, S_ROOT, :]))
            link(V.tensor_tensor(ST[:, S_SCALE, :], ST[:, S_SCALE, :], gamma, ALU.mult))
            mean = ST[:, S_MEAN:S_MEAN + 1, :].broadcast_to([P, NB, D])
            scale = ST[:, S_SCALE:S_SCALE + 1, :].broadcast_to([P, NB, D])
            link(V.tensor_tensor(H[:, :, :], H[:, :, :], over_b(2), ALU.add))
            link(V.tensor_tensor(H[:, :, :], H[:, :, :], mean, ALU.subtract))
            link(V.tensor_tensor(H[:, :, :], H[:, :, :], scale, ALU.mult))
            link(V.tensor_tensor(FEAT, H[:, :, :], over_b(4), ALU.add))
            loc_all = LOC[:, :].rearrange("a (g u) -> a g u", u=LPG)
            link(V.scalar_tensor_tensor(AT.rearrange("a (g u) -> a g u", u=LPG),
                                        first.broadcast_to([1, 2 * TRIPS, LPG]), float(P), loc_all, ALU.mult, ALU.add))
            link(V.tensor_scalar(LOC[:, :], LOC[:, :], 1, None, ALU.arith_shift_right))
            clear(SUMS)
            dve.wait_ge(group_added, (LAST_PASS + 1) * GK + 1)
            dve.sem_inc(bn_ready, 1)

            def edge_turned(g, h, i):
                dve.wait_ge(drow_in[h], i * 16 + 16)
                if static(g, 2):
                    dve.wait_ge(e_picked, g - 1)
                V.tensor_scalar(OTS[:, h, :, :], DROW[:, h, :, :], VIS[:, 0:1], None, ALU.is_equal
                                ).then_inc(e_turned, 1)

            def edge_onehots(g, h):
                onehots(DLOC[:, bass.ds(g * GRP, GRP)], h).then_inc(e_onehot, 1)

            def edge_act(g, h):
                dve.wait_ge(e_picked, g + 1)
                dve.wait_ge(e_scaled, g + 1)
                scaled = SCALED[:, h, :, :]
                V.tensor_tensor(scaled, scaled, ps_u[:, h, 0:GRP, :], ALU.add).then_inc(e_summed, 1)
                dve.wait_ge(e_summed, g + 1)
                if static(g, 2):
                    dve.wait_ge(e_product, g - 1)
                V.scalar_tensor_tensor(ACTED[:, h, :, :], scaled, SLOPE, scaled, ALU.mult, ALU.max
                                       ).then_inc(e_acted, 1)

            def edge_add(g, h):
                dve.wait_ge(e_product, g + 1)
                dve.sem_inc(dve_go, 1)
                add_group(LAST_PASS + 1, g, ps_s[:, h, :, :], D)

            for h in range(2):
                edge_turned(h, h, 0)
                edge_onehots(h, h)
            edge_act(0, 0)

            def edge_group(g, h, i):
                edge_act(g - 1, 1 - h)
                edge_turned(g, h, i)
                edge_add(g - 2, h)
                edge_onehots(g, h)
            with dve.Fori(1, TRIPS) as i:
                for h in range(2):
                    edge_group(2 * i + h, h, i)
            edge_act(2 * TRIPS - 1, 1)
            for h in range(2):
                edge_add(2 * TRIPS - 2 + h, h)
            dve.wait_ge(group_added, (LAST_PASS + 2) * GK)

            link(V.tensor_scalar(CNT[:, :], CNT[:, :], 1.0, None, ALU.max))
            link(V.reciprocal(CNT[:, :], CNT[:, :]))
            link(V.tensor_tensor(H[:, :, :], SUMS, over_f(CNT), ALU.mult))
            V.tensor_tensor(X[:, :, :], X[:, :, :], H[:, :, :], ALU.add).then_inc(result, 1)


def kernel(**inputs):
    import numpy as np
    import concourse.bacc as bacc
    from concourse.bass_utils import run_bass_kernel_spmd

    a = {k: np.asarray(v) for k, v in inputs.items()}
    xp = np.zeros((NB * P, D), np.float32)
    xp[:N] = a["x"]
    edges = np.full((3, ROWS * P), 0, np.int32)
    edges[0, E:] = FAR
    for k, name in enumerate(("dst", "src", "edge_type_4")):
        edges[k, :E] = a[name]
    arrays = {
        "x": np.ascontiguousarray(xp.reshape(NB, P, D).transpose(1, 0, 2)),
        "edges": np.ascontiguousarray(edges.reshape(3, ROWS, P).transpose(1, 0, 2)).reshape(ROWS, 3 * P),
        "dst": a["dst"],
        "L0_W1": a["L0_gnn_W1"], "L0_b1": a["L0_gnn_b1"], "L0_W2": a["L0_gnn_W2"], "L0_b2": a["L0_gnn_b2"],
        "L1_Wt": a["L1_gnn_W"].transpose(2, 0, 1).reshape(D, TYPES * D), "L1_b": a["L1_gnn_b"].reshape(1, TYPES * D),
        "L1_wih": a["L1_gnn_w_ih"].T, "L1_whh": a["L1_gnn_w_hh"].T,
        "L1_bih": a["L1_gnn_b_ih"].reshape(1, 3 * D), "L1_bhh": a["L1_gnn_b_hh"].reshape(1, 3 * D),
        "L2_W1": a["L2_gnn_W1"], "L2_b1": a["L2_gnn_b1"], "L2_W2": a["L2_gnn_W2"], "L2_b2": a["L2_gnn_b2"],
        "L3_Wt": a["L3_gnn_W"].T, "L3_b": a["L3_gnn_b"], "L3_gamma": a["L3_gnn_gamma"], "L3_beta": a["L3_gnn_beta"],
    }
    arrays = {k: np.ascontiguousarray(v) for k, v in arrays.items()}
    nc = bacc.Bacc("TRN2", target_bir_lowering=False, num_devices=1)
    args = {k: nc.dram_tensor(k, v.shape, mybir.dt.from_np(v.dtype), kind="ExternalInput").ap()
            for k, v in arrays.items()}
    out = nc.dram_tensor("out", (P, NB, D), F32, kind="ExternalOutput").ap()
    gnn_kernel(nc, out=out, **args)
    r = run_bass_kernel_spmd(nc, [arrays], core_ids=[0])
    return r.results[0]["out"].transpose(1, 0, 2).reshape(NB * P, D)[:N]
```

```python
from contextlib import ExitStack

import concourse.bass as bass
from concourse import mybir

F32 = mybir.dt.float32
I32 = mybir.dt.int32
BF16 = mybir.dt.bfloat16
ALU = mybir.AluOpType
ACT = mybir.ActivationFunctionType
AX_X = mybir.AxisListType.X

P = 128
N = 12500
E = 200000
D = 64
TYPES = 4
STEPS = 4
assert TYPES == 4
SLOPE = 0.3
EPS = 1e-5
NB = -(-N // P)
ROWS = -(-E // P)
VISITS = ROWS - 1 + NB
GRP = 10
TRIPS = VISITS // (2 * GRP)
RING = 12
BATCHES = -(-ROWS // GRP)
LAPS = ROWS // (GRP * RING)
RING_ROWS = RING * GRP
BATCH_OF = (1639, 14)
LAP_OF = (2185, 18)
RINGS = STEPS + 2
IN_BATCHES = [-(-BATCHES // 2), BATCHES // 2]
IN_ROWS = [ROWS - IN_BATCHES[1] * GRP, IN_BATCHES[1] * GRP]
VT = -(-VISITS // P)
CH = 2
NCH = NB // CH
GK = 2 * TRIPS + 1
STAT_CH = 14
STAT = -(-2 * TRIPS // STAT_CH) * STAT_CH
QUADS = -(-GRP // 4)
LPG = 4 * QUADS
LAST_PASS = 1 + STEPS + 2
RUN_MLP, RUN_TYPE, RUN_GRU, RUN_GCN, RUN_EDGE = 0, 1, 2, 1 + 2 * STEPS, 3 + 2 * STEPS
LOADS = 21
S_MEAN, S_VAR, S_ROOT, S_SCALE, S_SHIFT, S_TMP = range(6)
SLOT_DMAS = [16 * (NCH // 2 + 1), 16 * (NCH // 2)]
FAR = 1 << 20
assert BATCHES == LAPS * RING + 1 and RING % 2 == 0 and GRP * RING >= NB + 2 * GRP
assert all((k * BATCH_OF[0]) >> BATCH_OF[1] == k // GRP for k in range(ROWS))
assert all((k * LAP_OF[0]) >> LAP_OF[1] == k // RING_ROWS for k in range(ROWS))
assert VISITS == 2 * GRP * TRIPS and NCH * CH == NB and NCH % 2 == 1


def gnn_kernel(nc, x, edges, row_ends, L0_W1, L0_b1, L0_W2, L0_b2, L1_Wt, L1_b, L1_wih, L1_whh, L1_bih, L1_bhh,
               L2_W1, L2_b1, L2_W2, L2_b2, L3_Wt, L3_b, L3_gamma, L3_beta, out):
    def dram(name, shape, dt):
        return nc.dram_tensor(name, shape, dt).ap()

    tab_gin = dram("tab_gin", [P * NB, D], F32)
    tab_gated = dram("tab_gated", [P * NB * TYPES, D], F32)
    tab_gcn = [dram(f"tab_gcn{i}", [P * NB, D], F32) for i in range(2)]
    tab_edge = dram("tab_edge", [P * NB, D], F32)
    kept = dram("kept", [P, VISITS, D], F32)
    blk_dram = dram("blk_dram", [VT, P], I32)
    dloc_dram = dram("dloc_dram", [VT * P, P], BF16)

    with ExitStack() as ctx:
        def sb(name, shape, dt=F32):
            return ctx.enter_context(nc.sbuf_tensor(name, shape, dt))

        def sem(name):
            return ctx.enter_context(nc.semaphore(name))

        ps = ctx.enter_context(nc.psum_tensor("ps", [P, 4096], F32))

        X = sb("X", [P, NB, D])
        HG = sb("HG", [P, NB * D + 2 * GRP * P])
        Hf, Gf = HG[:, 0:NB * D], HG[:, NB * D:]
        H = Hf.rearrange("p (b f) -> p b f", f=D)
        G = Gf.rearrange("p (h u f) -> p h u f", h=2, u=GRP)
        RINGF = HG[:, 0:RING_ROWS * D]
        A = sb("A", [P, NB * P])
        A3 = A[:, :].rearrange("p (b f) -> p b f", f=P)
        SUMS, FEAT = A3[:, :, 0:D], A3[:, :, D:P]
        DLOC = sb("DLOC", [P, VT * P])
        IDX = sb("IDX", [P, VT * P], I32)
        IDX4 = sb("IDX4", [P, VT * P], I32)
        LOC = sb("LOC", [1, 2 * TRIPS * LPG], I32)
        SLOT = sb("SLOT", [1, 2 * TRIPS * LPG], I32)
        FIRST = sb("FIRST", [1, 2 * TRIPS], I32)
        ZERO = sb("ZERO", [1, 512], BF16)
        STG = sb("STG", [P, 2, GRP], I32)
        OH = sb("OH", [P, 2, GRP, P])
        CNT = sb("CNT", [P, NB])
        DINV = sb("DINV", [P, NB])
        SA = sb("SA", [P, NB])
        SB = sb("SB", [P, NB])
        SC = sb("SC", [P, NB])
        IDENT = sb("IDENT", [P, P])
        IOTAR = sb("IOTAR", [P, P])
        VIS = sb("VIS", [P, VT])
        BND = sb("BND", [P, NB])
        ENDS = sb("ENDS", [P, VT], I32)
        ENDF = sb("ENDF", [P, VT])
        CNTB = sb("CNTB", [P, NB])
        TS = sb("TS", [P, NB])
        IOB = sb("IOB", [P, NB])
        BJ = sb("BJ", [P, VT])
        BJ128 = sb("BJ128", [P, VT])
        TJF = sb("TJF", [P, VT])
        TJ = sb("TJ", [P, VT], I32)
        BT = sb("BT", [VT, P], I32)
        ONES = sb("ONES", [P, P])
        EPSC = sb("EPSC", [P, 1])
        PICK = sb("PICK", [P, 2, CH, P])
        XT = sb("XT", [D + 1, 2, CH * P])
        XG = sb("XG", [P, 2, CH * P])
        R1 = sb("R1", [D + 1, 2, CH * P])
        RZ = sb("RZ", [P, 2, CH, P])
        NN = sb("NN", [P, 2, CH, D])
        DZ = sb("DZ", [P, 2, CH, D])
        TW = sb("TW", [P, 2, CH * TYPES * D])
        WG = sb("WG", [P, 4 * D])
        BG = sb("BG", [1, 2, 4 * D])
        BG3 = sb("BG3", [D + 1, CH * 4 * D], BF16)
        ONE16 = sb("ONE16", [D + 1, P], BF16)
        WT = sb("WT", [D + 1, TYPES * D])
        W01 = sb("W01", [D, D])
        B01 = sb("B01", [D, 1])
        W02 = sb("W02", [D + 1, D])
        W2 = sb("W2", [D, 2, D])
        W3 = sb("W3", [D, 2, D])
        W3A = sb("W3A", [D, D])
        BC = sb("BC", [P, 5, D])
        ST = sb("ST", [P, 6, D])

        Af = A[:, :]
        n3 = VT * 3 * P
        F3 = Af[:, 0:n3].rearrange("p (k g e) -> p k g e", g=VT, k=3)
        EB = Af[:, n3:2 * n3].bitcast(I32).rearrange("p (g k e) -> p g k e", g=VT, k=3)
        SQ0 = Af[:, n3:n3 + NB * D].rearrange("p (b f) -> p b f", f=D)
        OHf = OH[:, :, :, :].rearrange("p a u e -> p (a u e)")
        SLO = Gf[:, 0:VT * P].bitcast(I32).rearrange("p (g e) -> p g e", g=VT)
        SHI = OHf[:, 0:VT * P].bitcast(I32).rearrange("p (g e) -> p g e", g=VT)
        na = n3 + n3
        SRC = F3[:, 2, :, :].bitcast(I32)
        TYP = Af[:, na:na + VT * P].bitcast(I32).rearrange("p (g e) -> p g e", g=VT)
        RLO, RHI = (t[:, :].rearrange("p (g e) -> p g e", g=VT) for t in (IDX, IDX4))
        BLK = OHf[0:1, 0:VT * P].bitcast(I32)
        VNUM, VROW, VTMP = (Af[0:1, k * VISITS:(k + 1) * VISITS].bitcast(I32).rearrange("a (g u) -> a g u", u=GRP)
                            for k in range(3))
        BELOW = Hf[:, 0:NB * VT].rearrange("p (b j) -> p b j", j=VT)

        DL16 = OHf[:, VT * P:VT * P + VT * P // 2].bitcast(BF16).rearrange("p (g e) -> p g e", g=VT)

        na = VT * P
        MASK = Af[:, 0:na]
        AT = Af[0:1, na:na + 2 * TRIPS * LPG].bitcast(I32)
        na += 2 * TRIPS * LPG
        OTS = Af[:, na:na + 2 * GRP * P].rearrange("p (h u e) -> p h u e", h=2, u=GRP)
        na += 2 * GRP * P
        DROW = Af[:, na:na + GRP * P].bitcast(BF16).rearrange("p (h u e) -> p h u e", h=2, u=GRP)
        na += GRP * P
        TOTAL = Af[:, na:na + P]

        LOADED = Gf[:, 0:2 * GRP * D].rearrange("p (h u f) -> p h u f", h=2, u=GRP)
        SCALED = Gf[:, 2 * GRP * D:4 * GRP * D].rearrange("p (h u f) -> p h u f", h=2, u=GRP)
        ACTED = Hf[:, 0:2 * GRP * D].rearrange("p (h u f) -> p h u f", h=2, u=GRP)

        ps_g = ps[:, 0:3072].rearrange("p (h u f) -> p h u f", h=2, f=P)
        ps_t = ps[:, 0:1024].rearrange("p (s f) -> p s f", s=2)
        ps_o = ps[:, 1024:2048].rearrange("p (s f) -> p s f", s=2)
        ps_u = ps[:, 0:2048].rearrange("p (h u f) -> p h u f", h=2, f=D)
        ps_s = ps[:, 2048:4096].rearrange("p (h u f) -> p h u f", h=2, f=D)
        ps_stat = ps[:, 2048:2048 + STAT]
        ps_m = ps[:, 2048:3072].rearrange("p (s f) -> p s f", s=2)


        ps_gate = ps_o.rearrange("p s (c f) -> p s c f", c=CH)
        ps_vu = ps_o[:, :, 0:CH * P].rearrange("p s (c f) -> p s c f", c=CH)
        ps_x = ps_o[:, :, 0:CH * D].rearrange("p s (c f) -> p s c f", c=CH)
        tw_v = TW[:, :, 0:CH * D].rearrange("p s (c f) -> p s c f", c=CH)

        ends_in, x_in, w_in = sem("ends_in"), sem("x_in"), sem("w_in")
        iota_done = sem("iota_done")
        dve_done = sem("dve_done")
        below = sem("below")
        totals = sem("totals")
        rows_known = sem("rows_known")
        rows_in = sem("rows_in")
        cols_done = sem("cols_done")
        turned = sem("turned")
        tabled = sem("tabled")
        blk_out, blk_in = sem("blk_out"), sem("blk_in")
        vnum_set = sem("vnum_set")
        loc_set = sem("loc_set")
        dloc_cast, dloc_out = sem("dloc_cast"), sem("dloc_out")

        centred, squared = sem("centred"), sem("squared")
        varred, rooted = sem("varred"), sem("rooted")
        normed = sem("normed")

        batch_in = sem("batch_in")
        typ_in = sem("typ_in")
        staged = [sem(f"staged{h}") for h in range(2)]
        pool_go = sem("pool_go")
        pe_go = sem("pe_go")
        dve_go = sem("dve_go")
        rows_gated = [sem(f"rows_gated{h}") for h in range(2)]
        rows_other = [sem(f"rows_other{h}") for h in range(2)]
        onehot = [sem(f"onehot{h}") for h in range(2)]
        product = [sem(f"product{h}") for h in range(2)]
        group_added = sem("group_added")
        table_out = sem("table_out")
        chunk_picked = sem("chunk_picked")
        chunk_turned = sem("chunk_turned")
        chunk_copied = sem("chunk_copied")
        chunk_made = sem("chunk_made")
        mlp_in = sem("mlp_in")
        mlp_mid, mlp_act = sem("mlp_mid"), sem("mlp_act")
        mlp_done = sem("mlp_done")
        typ_dve, typ_act = sem("typ_dve"), sem("typ_act")
        typ_out = [sem(f"typ_out{s}") for s in range(2)]
        gru_sig, gru_tanh = sem("gru_sig"), sem("gru_tanh")
        gru_pre, gru_out = sem("gru_pre"), sem("gru_out")
        idx_shifted = sem("idx_shifted")
        root_deg, gcn_done, gcn_in = sem("root_deg"), sem("gcn_done"), sem("gcn_in")
        edg_v, edg_u = sem("edg_v"), sem("edg_u")
        edg_out = [sem(f"edg_out{s}") for s in range(2)]
        kept_out = [sem(f"kept_out{h}") for h in range(2)]
        stat_wide, stat_sum, stat_var, stat_root = (sem(f"stat_{n}") for n in ("wide", "sum", "var", "root"))
        bn_ready = sem("bn_ready")
        kept_in = [sem(f"kept_in{h}") for h in range(2)]
        drow_in = [sem(f"drow_in{h}") for h in range(2)]
        mask_set = sem("mask_set")
        e_turned, e_picked, e_joined, e_squared, e_times, e_scaled, e_onehot, e_acted, e_product = (
            sem(f"e_{n}") for n in ("turned", "picked", "joined", "squared", "times", "scaled", "onehot",
                                    "acted", "product"))
        result, stored = sem("result"), sem("stored")

        block = ctx.enter_context(nc.Block())

        def staged_before(ring, h, after=1):
            return ring * IN_BATCHES[h] + after * TRIPS

        def rows_before(ring, h, by_visit):
            return ring * (16 * IN_ROWS[h]) + by_visit * (16 * GRP * TRIPS)

        def chunks(eng, *parts):
            def turn_of(r, i):
                for lag, part in enumerate(parts):
                    c = r - lag
                    if i is None and 0 <= c < NCH:
                        part(c, c % 2, c // 2)
                    elif i is not None:
                        part(2 * i + c, c % 2, i + c // 2)

            i_first = -(-(1 + len(parts)) // 2)
            for j in range(2 * i_first):
                turn_of(j, None)
            with eng.Fori(i_first, NCH // 2) as i:
                for r in range(2):
                    turn_of(r, i)
            for j in range(2 * (NCH // 2), NCH + len(parts) - 1):
                turn_of(j, None)

        def groups(eng, body):
            for h in range(2):
                body(0, h, True)
            with eng.Fori(1, TRIPS) as i:
                for h in range(2):
                    body(i, h, False)

        def groups_apart(eng, body):
            for h in range(2):
                body(h, h, 0)
            with eng.Fori(1, TRIPS) as i:
                for h in range(2):
                    body(2 * i + h, h, i)

        def static(v, least=1):
            return not isinstance(v, int) or v >= least

        def group_cols(t, i, h):
            return t[:, bass.ds(i * (2 * GRP) + h * GRP, GRP)]

        def two(t, c):
            return t[:, bass.ds(c * CH, CH), :]

        def table_rows(t, r):
            return t.rearrange("(p c r) f -> p c (r f)", p=P, c=NCH)

        @block.sync
        def _(sp):
            sp.dma_start(ENDS[:, :], row_ends).then_inc(ends_in, 16)
            by_row = edges.rearrange("(g p) (k e) -> p g k e", p=P, k=3)
            sp.dma_start(SRC, by_row[:, :, 1, :]).then_inc(typ_in, 16)
            sp.dma_start(TYP, by_row[:, :, 2, :]).then_inc(typ_in, 16)
            sp.dma_start(X[:, :, :], x).then_inc(x_in, 16)
            loads = [(W01[:, :], L0_W1), (B01[:, :], L0_b1.rearrange("(p a) -> p a", a=1)),
                     (W02[0:D, :], L0_W2), (W02[D:D + 1, :], L0_b2.rearrange("(a n) -> a n", a=1)),
                     (WT[0:D, :], L1_Wt), (WT[D:D + 1, :], L1_b),
                     (WG[0:D, 0:3 * D], L1_wih), (WG[D:P, 0:2 * D], L1_whh[:, 0:2 * D]),
                     (WG[D:P, 3 * D:4 * D], L1_whh[:, 2 * D:3 * D]),
                     (BG[:, 0, 0:3 * D], L1_bih), (BG[:, 1, 0:2 * D], L1_bhh[:, 0:2 * D]),
                     (BG[:, 1, 3 * D:4 * D], L1_bhh[:, 2 * D:3 * D]),
                     (W2[:, 0, :], L2_W1), (W2[:, 1, :], L2_W2),
                     (W3A[:, :], L3_Wt[0:D, :]), (W3[:, 0, :], L3_Wt[D:P, :])]
            loads += [(BC[:, k, :], r.partition_broadcast(P)) for k, r in
                      enumerate((L2_b1, L2_b2, L3_b, L3_gamma, L3_beta))]
            assert len(loads) == LOADS
            for o, i in loads:
                sp.dma_start(o, i).then_inc(w_in, 16)

            sp.wait_ge(dloc_cast, 1)
            sp.dma_start(dloc_dram.rearrange("(g p) e -> p g e", p=P), DL16).then_inc(dloc_out, 16)

            sp.wait_ge(tabled, 4)
            sp.dma_start(blk_dram, BT[:, :]).then_inc(blk_out, 16)
            sp.wait_ge(blk_out, 16)
            sp.dma_start(BLK, blk_dram.rearrange("g (a e) -> a (g e)", a=1)).then_inc(blk_in, 16)

            sp.wait_ge(normed, 1)
            sp.dma_start(tab_gin.rearrange("(p b) f -> p b f", p=P), H[:, :, :]).then_inc(table_out, 16)

            gated = table_rows(tab_gated, CH * TYPES)
            with sp.Fori(0, STEPS) as step:
                def send(c, s, i):
                    sp.wait_ge(typ_dve, step * NCH + c + 1)
                    sp.wait_ge(typ_act, step * NCH + c + 1)
                    sp.dma_start(gated[:, bass.ds(c, 1), :], TW[:, s:s + 1, :]).then_inc(typ_out[s], 16)
                chunks(sp, send)

            for k in range(2):
                conv = tab_gcn[k].rearrange("(p b) f -> p b f", p=P)

                def send_conv(c, s, i):
                    sp.wait_ge(gcn_done, k * NCH + c + 1)
                    sp.dma_start(two(conv, c), two(FEAT, c)).then_inc(table_out, 16)
                chunks(sp, send_conv)

            edge = table_rows(tab_edge, CH)

            def send_edge(c, s, i):
                sp.wait_ge(edg_v, c + 1)
                sp.dma_start(edge[:, bass.ds(c, 1), :], TW[:, s:s + 1, 0:CH * D]).then_inc(edg_out[s], 16)
            chunks(sp, send_edge)

            def load_row(g, h):
                sp.dma_start(DROW[:, h, :, :].rearrange("p u e -> p (u e)"),
                             dloc_dram[bass.ds(g * GRP, GRP), :].rearrange("u e -> (u e)").partition_broadcast(P)
                             ).then_inc(drow_in[h], 16)

            def keep(g, h, i):
                sp.wait_ge(e_joined, g + 1)
                sp.dma_start(kept[:, bass.ds(g * GRP, GRP), :], G[:, h, :, 0:D]).then_inc(kept_out[h], 16)

            def load_and_keep(g, h, i):
                sp.wait_ge(e_turned, g - 1)
                load_row(g, h)
                keep(g - 2, h, i)
            sp.wait_ge(mask_set, 1)
            for h in range(2):
                load_row(h, h)
            with sp.Fori(1, TRIPS) as i:
                for h in range(2):
                    load_and_keep(2 * i + h, h, i)
            for h in range(2):
                keep(2 * TRIPS - 2 + h, h, TRIPS - 1)
            for h in range(2):
                sp.wait_ge(kept_out[h], TRIPS * 16)

            sp.wait_ge(bn_ready, 1)

            def load_kept(g, h, i):
                if static(g, 2):
                    sp.wait_ge(e_times, g - 1)
                sp.dma_start(LOADED[:, h, :, :], kept[:, bass.ds(g * GRP, GRP), :]).then_inc(kept_in[h], 16)
            groups_apart(sp, load_kept)
            sp.wait_ge(result, 1)
            sp.dma_start(out, X[:, :, :]).then_inc(stored, 16)
            sp.wait_ge(stored, 16)

        @block.gpsimd
        def _(pool):
            kw = dict(allow_small_or_imprecise_dtypes=True)
            nc.gpsimd.iota(IOTAR[:, :], [[1, P]], base=0, channel_multiplier=0, **kw).then_inc(iota_done, 1)
            nc.gpsimd.iota(VIS[:, :], [[P, VT]], base=0, channel_multiplier=1, **kw).then_inc(iota_done, 1)
            nc.gpsimd.iota(BND[:, :], [[P, NB]], base=P, channel_multiplier=0, **kw).then_inc(iota_done, 1)
            nc.gpsimd.iota(IOB[:, :], [[1, NB]], base=1, channel_multiplier=0, **kw).then_inc(iota_done, 1)
            pool.wait_ge(rows_known, 1)
            for g in range(VT):
                nc.gpsimd.indirect_dma_start(
                    out=EB[:, g, :, :].rearrange("p k e -> p (k e)"), out_offset=None, in_=edges,
                    in_offset=bass.IndirectOffsetOnAxis(ap=TJ[:, g:g + 1], axis=0)).then_inc(rows_in, 16)

            def gather(n, table, rows, kept_):
                def body(i, h, first):
                    pool.wait_ge(staged[h], staged_before(0 if n == 0 else RINGS, h, min(n, 1)) + i + 1)
                    pool.sem_inc(pool_go, 1)
                    if kept_ and not first:
                        pool.wait_ge(kept_out[h], i * 16)
                        pool.sem_inc(pool_go, 1)
                    for u in range(GRP):
                        nc.gpsimd.indirect_dma_start(
                            out=G[:, h, u, 0:D], out_offset=None, in_=table,
                            in_offset=bass.IndirectOffsetOnAxis(ap=STG[:, h, u:u + 1], axis=0)
                        ).then_inc(rows[h], 16)
                groups(pool, body)

            def gather_ring(n, ring, table, rows):
                def batch(lap, j, count):
                    h = j % 2
                    i = lap * (RING // 2) + j // 2
                    pool.wait_ge(product[h], n * TRIPS + i)
                    pool.sem_inc(pool_go, 1)
                    pool.wait_ge(staged[h], staged_before(ring, h) + i + 1)
                    pool.sem_inc(pool_go, 1)
                    for u in range(count):
                        at = (j * GRP + u) * D
                        nc.gpsimd.indirect_dma_start(
                            out=RINGF[:, at:at + D], out_offset=None, in_=table,
                            in_offset=bass.IndirectOffsetOnAxis(ap=STG[:, h, u:u + 1], axis=0)
                        ).then_inc(rows[h], 16)
                with pool.Fori(0, LAPS) as lap:
                    for j in range(RING):
                        batch(lap, j, GRP)
                batch(LAPS, 0, ROWS - LAPS * RING_ROWS)

            def pick(run, src, width, plus=None):
                def body(c, s, i):
                    if static(i):
                        pool.wait_ge(chunk_turned, run * NCH + c - 1)
                        pool.sem_inc(pool_go, 1)
                    to = PICK[:, s, :, 0:width]
                    if plus is None:
                        nc.gpsimd.tensor_copy(to, two(src, c)).then_inc(chunk_picked, 1)
                    else:
                        nc.gpsimd.tensor_tensor(to, two(src, c), two(plus, c), ALU.add).then_inc(chunk_picked, 1)
                chunks(pool, body)

            pool.wait_ge(tabled, 4)
            nc.gpsimd.iota(VNUM, [[GRP, 2 * TRIPS], [1, GRP]], base=0, channel_multiplier=0).then_inc(vnum_set, 1)
            pool.wait_ge(table_out, 16)
            gather(0, tab_gin, rows_other, False)
            pool.wait_ge(mlp_in, 1)
            pick(RUN_MLP, H, D, plus=SUMS)
            with pool.Fori(0, STEPS) as step:
                pool.wait_ge(group_added, (step + 1) * GK + 1)
                pool.sem_inc(pool_go, 1)
                pick(2 * step + RUN_TYPE, FEAT, D)
                for s in range(2):
                    pool.wait_ge(typ_out[s], (step + 1) * SLOT_DMAS[s])
                    pool.sem_inc(pool_go, 1)
                gather_ring(step + 1, step, tab_gated, rows_gated)
                pool.wait_ge(group_added, (step + 2) * GK)
                pool.sem_inc(pool_go, 1)
                pick(2 * step + RUN_GRU, A3, P)
            for k in range(2):
                pool.wait_ge(gcn_in, k + 1)
                pick(RUN_GCN + k, H, D)
                pool.wait_ge(table_out, 16 + (k + 1) * 16 * NCH)
                gather_ring(STEPS + 1 + k, STEPS + k, tab_gcn[k], rows_other)
            pool.wait_ge(normed, 4)
            pick(RUN_EDGE, H, D)
            for s in range(2):
                pool.wait_ge(edg_out[s], SLOT_DMAS[s])
            gather(LAST_PASS, tab_edge, rows_other, True)

            scale = ST[:, S_SCALE:S_SCALE + 1, :].broadcast_to([P, GRP, D])
            shift = ST[:, S_SHIFT:S_SHIFT + 1, :].broadcast_to([P, GRP, D])
            pool.wait_ge(bn_ready, 1)

            def scale_rows(g, h, i):
                pool.wait_ge(kept_in[h], i * 16 + 16)
                pool.sem_inc(pool_go, 1)
                if static(g, 2):
                    pool.wait_ge(e_acted, g - 1)
                    pool.sem_inc(pool_go, 1)
                scaled = SCALED[:, h, :, :]
                nc.gpsimd.tensor_tensor(scaled, LOADED[:, h, :, :], scale, ALU.mult).then_inc(e_times, 1)
                pool.wait_ge(e_times, g + 1)
                pool.sem_inc(pool_go, 1)
                nc.gpsimd.tensor_tensor(scaled, scaled, shift, ALU.add).then_inc(e_scaled, 1)
            groups_apart(pool, scale_rows)

        @block.scalar
        def _(act):
            def square_all(n, squares):
                act.wait_ge(centred, n + 1)
                nc.scalar.activation(squares, H[:, :, :], ACT.Square).then_inc(squared, 1)

            def root(n):
                act.wait_ge(varred, n + 1)
                nc.scalar.activation(SB[:, :], SA[:, :], ACT.Sqrt, bias=EPSC[:, 0:1], scale=1.0 / D
                                     ).then_inc(rooted, 1)

            def norm(n):
                square_all(n, SUMS)
                root(n)

            act.wait_ge(cols_done, 1)
            nc.scalar.copy(DL16, F3[:, 0, :, :]).then_inc(dloc_cast, 1)

            square_all(0, SQ0)

            for k, table in enumerate((DLOC, IDX, IDX4)):
                act.wait_ge(turned, k + 1)
                half = 2048 * (k % 2)
                nc.scalar.copy(table[:, :], ps[:, half:half + VT * P]).then_inc(tabled, 1)
            act.wait_ge(turned, 4)
            nc.scalar.copy(BT[:, :], ps[0:VT, 2048:2048 + P]).then_inc(tabled, 1)

            def stage_indices(n, table):
                def body(i, h, first):
                    if not first:
                        act.wait_ge(product[h], n * TRIPS + i)
                    nc.scalar.copy(STG[:, h, :], group_cols(table, i, h)).then_inc(staged[h], 1)
                groups(act, body)

            root(0)
            act.wait_ge(tabled, 4)
            stage_indices(0, IDX)

            def stage_batches(rows, before):
                def come(h, rows_):
                    act.wait_ge(rows[h], before(h) + rows_ * 16)
                    act.sem_inc(batch_in, 1)

                def stage(i, h):
                    nc.scalar.copy(STG[:, h, :], group_cols(IDX4, i, h)).then_inc(staged[h], 1)
                for h in range(2):
                    stage(0, h)
                with act.Fori(1, BATCHES // 2) as i:
                    for h in range(2):
                        come(h, i * GRP)
                        stage(i, h)
                come(0, IN_ROWS[1])
                stage(BATCHES // 2, 0)
                come(1, IN_ROWS[1])
                come(0, IN_ROWS[0])

            def copied(run, dst, rows):
                def part(c, s, i):
                    act.wait_ge(chunk_turned, run * NCH + c + 1)
                    nc.scalar.copy(dst[0:rows, s, :], ps_t[0:rows, s, 0:CH * P]).then_inc(chunk_copied, 1)
                return part

            def mlp_relu(c, s, i):
                act.wait_ge(mlp_mid, c + 1)
                nc.scalar.activation(R1[0:D, s, :], ps_m[0:D, s, 0:CH * P], ACT.Relu, bias=B01[:, 0:1]
                                     ).then_inc(mlp_act, 1)
            chunks(act, copied(RUN_MLP, XT, D), mlp_relu)

            norm(1)

            with act.Fori(0, STEPS) as step:
                def type_chunk(c, s, i):
                    act.wait_ge(chunk_made, (2 * step + RUN_TYPE) * NCH + c + 1)
                    if static(i):
                        act.wait_ge(typ_out[s], step * SLOT_DMAS[s] + i * 16)
                    nc.scalar.copy(TW[:, s, 0:TYPES * D], ps_o[:, s, 0:TYPES * D]).then_inc(typ_act, 1)
                chunks(act, copied(2 * step + RUN_TYPE, XT, D), type_chunk)
                stage_batches(rows_gated, lambda h: rows_before(step, h, 0))

                def gru_sigmoid(c, s, i):
                    act.wait_ge(chunk_made, (2 * step + RUN_GRU) * NCH + c + 1)
                    if static(i):
                        act.wait_ge(gru_out, step * (NCH * 3) + (c - 1) * 3)
                    nc.scalar.activation(RZ[:, s, :, :], ps_gate[:, s, :, 0:2 * D], ACT.Sigmoid).then_inc(gru_sig, 1)

                def gru_tanh_n(c, s, i):
                    act.wait_ge(gru_pre, step * (NCH * 2) + c * 2 + 2)
                    nc.scalar.activation(NN[:, s, :, :], NN[:, s, :, :], ACT.Tanh).then_inc(gru_tanh, 1)
                chunks(act, copied(2 * step + RUN_GRU, XG, P), gru_sigmoid, gru_tanh_n)

            act.wait_ge(normed, 2)
            nc.scalar.activation(SC[:, :], CNT[:, :], ACT.Sqrt, bias=ONES[:, 0:1]).then_inc(root_deg, 1)
            norm(2)
            for k in range(2):
                chunks(act, copied(RUN_GCN + k, XT, D))
                if k == 0:
                    act.wait_ge(idx_shifted, 1)
                stage_batches(rows_other, lambda h: rows_before(k, h, 1))

            norm(3)

            chunks(act, copied(RUN_EDGE, XT, D))

            def stage_last(i, h):
                nc.scalar.copy(STG[:, h, :], group_cols(IDX, i, h)).then_inc(staged[h], 1)

            def square(g, h):
                act.wait_ge(e_joined, g + 1)
                nc.scalar.activation(G[:, h, :, D:P], G[:, h, :, 0:D], ACT.Square).then_inc(e_squared, 1)

            for h in range(2):
                act.wait_ge(product[h], LAST_PASS * TRIPS)
                stage_last(0, h)
            with act.Fori(1, TRIPS) as i:
                for h in range(2):
                    square(2 * i + (h - 2), h)
                    act.wait_ge(product[h], LAST_PASS * TRIPS + i)
                    stage_last(i, h)
            for h in range(2):
                square(2 * TRIPS - 2 + h, h)

            act.wait_ge(stat_var, 1)
            nc.scalar.activation(ST[:, S_ROOT, :], ST[:, S_VAR, :], ACT.Sqrt, bias=EPSC[:, 0:1]).then_inc(stat_root, 1)

        @block.tensor
        def _(pe):
            pe.wait_ge(below, 1)
            nc.tensor.matmul(ps[:, 0:NB], ONES[:, :], CNTB[:, :], start=True, stop=True).then_inc(totals, 1)

            pe.wait_ge(cols_done, 1)
            for k in range(3):
                if k == 2:
                    pe.wait_ge(tabled, 1)
                half = 2048 * (k % 2)
                for g in range(VT):
                    ins = nc.tensor.transpose(ps[:, half + g * P:half + (g + 1) * P], F3[:, k, g, :], IDENT[:, :])
                ins.then_inc(turned, 1)
            pe.wait_ge(tabled, 2)
            nc.tensor.transpose(ps[0:VT, 2048:2048 + P], BJ128[:, :], IDENT[:, :]).then_inc(turned, 1)

            def load_places(table, g, most):
                places = []
                for q in range(QUADS):
                    _, regs = nc.values_load_multi_w_load_instructions(
                        table[0:1, bass.ds(g * LPG + 4 * q, 4)], engines=[mybir.EngineType.PE], min_val=0,
                        max_val=most, skip_runtime_bounds_check_because="at most ten blocks in a group")
                    places += list(regs)
                return places[:GRP]

            def zero(base, columns):
                for b in range(0, columns, 512):
                    w = min(512, columns - b)
                    nc.tensor.matmul(ps[:, base + b:base + b + w], ZERO[:, 0:P], ZERO[:, 0:w], start=True, stop=True)

            def accumulate(base, place, width, onehots_, rows_):
                return nc.tensor.matmul(ps[:, base:][:, bass.ds(place, width)], onehots_, rows_, start=False,
                                        stop=False, skip_group_check=True)

            def products(n, width, rows):
                def body(i, h, first):
                    base = h * 1536
                    places = load_places(LOC, 2 * i + h, (GRP - 1) * P)
                    if not first:
                        pe.wait_ge(group_added, n * GK + 2 * i + h)
                        pe.sem_inc(pe_go, 1)
                    zero(base, GRP * P)
                    pe.wait_ge(onehot[h], n * TRIPS + i + 1)
                    pe.wait_ge(rows[h], (i + 1) * (16 * GRP))
                    for u in range(GRP):
                        ins = accumulate(base, places[u], width, OH[:, h, u, :], G[:, h, u, 0:width])
                    ins.then_inc(product[h], 1)
                groups(pe, body)

            def ring_products(n, ring):
                def body(i, h, first):
                    base = h * 1536
                    places = load_places(LOC, 2 * i + h, (GRP - 1) * P)
                    slots = load_places(SLOT, 2 * i + h, (RING_ROWS - 1) * D)
                    needed = pe.value_load(LOC[0:1, bass.ds((2 * i + h) * LPG + GRP, 1)], min_val=1,
                                           max_val=BATCHES)
                    if not first:
                        pe.wait_ge(group_added, n * GK + 2 * i + h)
                        pe.sem_inc(pe_go, 1)
                    zero(base, GRP * P)
                    pe.wait_ge(onehot[h], n * TRIPS + i + 1)
                    pe.wait_ge(batch_in, ring * BATCHES + needed)
                    for u in range(GRP):
                        ins = accumulate(base, places[u], D, OH[:, h, u, :], RINGF[:, bass.ds(slots[u], D)])
                    ins.then_inc(product[h], 1)
                groups(pe, body)

            def turn(run, width):
                def part(c, s, i):
                    pe.wait_ge(chunk_picked, run * NCH + c + 1)
                    pe.sem_inc(pe_go, 1)
                    for k in range(CH):
                        ins = nc.tensor.transpose(ps_t[0:width, s, k * P:(k + 1) * P], PICK[:, s, k, 0:width],
                                                  IDENT[:, :])
                    ins.then_inc(chunk_turned, 1)
                return part

            pe.wait_ge(tabled, 4)
            pe.wait_ge(loc_set, 1)
            products(0, D + 1, rows_other)

            pe.wait_ge(w_in, 16 * LOADS)
            pe.wait_ge(mlp_in, 1)

            def mlp_hidden(c, s, i):
                pe.wait_ge(chunk_copied, RUN_MLP * NCH + c + 1)
                pe.sem_inc(pe_go, 1)
                nc.tensor.matmul(ps_m[0:D, s, 0:CH * P], W01[:, :], XT[0:D, s, :], start=True, stop=True
                                 ).then_inc(mlp_mid, 1)

            def mlp_out(c, s, i):
                pe.wait_ge(mlp_act, c + 1)
                if static(i):
                    pe.wait_ge(mlp_done, c - 1)
                for k in range(CH):
                    ins = nc.tensor.matmul(ps_x[:, s, k, :], R1[:, s, k * P:(k + 1) * P], W02[:, :],
                                           start=True, stop=True)
                ins.then_inc(chunk_made, 1)
            chunks(pe, turn(RUN_MLP, D), mlp_hidden, mlp_out)

            with pe.Fori(0, STEPS) as step:
                def type_chunk(c, s, i):
                    pe.wait_ge(chunk_copied, (2 * step + RUN_TYPE) * NCH + c + 1)
                    if static(i):
                        pe.wait_ge(typ_dve, step * NCH + c - 1)
                        pe.wait_ge(typ_act, step * NCH + c - 1)
                    for k, bank in enumerate((ps_o, ps_m)):
                        ins = nc.tensor.matmul(bank[:, s, 0:TYPES * D], XT[:, s, k * P:(k + 1) * P], WT[:, :],
                                               start=True, stop=True)
                    ins.then_inc(chunk_made, 1)
                chunks(pe, turn(2 * step + RUN_TYPE, D), type_chunk)
                pe.wait_ge(typ_dve, (step + 1) * NCH)
                pe.wait_ge(typ_act, (step + 1) * NCH)
                pe.sem_inc(pe_go, 1)
                ring_products(step + 1, step)

                pe.wait_ge(group_added, (step + 2) * GK)

                def gru_chunk(c, s, i):
                    pe.wait_ge(chunk_copied, (2 * step + RUN_GRU) * NCH + c + 1)
                    if static(i):
                        pe.wait_ge(gru_pre, step * (NCH * 2) + (c - 1) * 2)
                    nc.tensor.matmul(ps_o[:, s, :], ONE16[:, :], BG3[:, :], start=True, stop=True)
                    for k in range(CH):
                        ins = nc.tensor.matmul(ps_gate[:, s, k, :], XG[:, s, k * P:(k + 1) * P], WG[:, :],
                                               start=False, stop=False, skip_group_check=True)
                    ins.then_inc(chunk_made, 1)
                chunks(pe, turn(2 * step + RUN_GRU, P), gru_chunk)
                pe.wait_ge(gru_pre, (step + 1) * (NCH * 2))

            for n in range(2):
                def gcn_chunk(c, s, i):
                    pe.wait_ge(chunk_copied, (RUN_GCN + n) * NCH + c + 1)
                    if static(i):
                        pe.wait_ge(gcn_done, n * NCH + c - 1)
                    for k in range(CH):
                        ins = nc.tensor.matmul(ps_x[:, s, k, :], XT[0:D, s, k * P:(k + 1) * P], W2[:, n, :],
                                               start=True, stop=True)
                    ins.then_inc(chunk_made, 1)
                chunks(pe, turn(RUN_GCN + n, D), gcn_chunk)
                pe.wait_ge(gcn_done, (n + 1) * NCH)
                ring_products(STEPS + 1 + n, STEPS + n)
                pe.wait_ge(group_added, (STEPS + 2 + n) * GK)

            def edge_chunk(c, s, i):
                pe.wait_ge(chunk_copied, RUN_EDGE * NCH + c + 1)
                if static(i):
                    pe.wait_ge(edg_u, c - 1)
                for k in range(CH):
                    ins = nc.tensor.matmul(ps_vu[:, s, k, :], XT[0:D, s, k * P:(k + 1) * P],
                                           W3[:, :, :].rearrange("p a f -> p (a f)"), start=True, stop=True)
                ins.then_inc(chunk_made, 1)
            chunks(pe, turn(RUN_EDGE, D), edge_chunk)
            pe.wait_ge(edg_u, NCH)

            pe.wait_ge(mask_set, 1)
            zero(2048, 512)

            def pick_u(g, h):
                at = load_places(AT, g, (NB - 1) * D)
                pe.wait_ge(e_turned, g + 1)
                if static(g, 2):
                    pe.wait_ge(e_joined, g - 1)
                for u in range(GRP):
                    ins = nc.tensor.matmul(ps_u[:, h, u, :], OTS[:, h, u, :], Hf[:, bass.ds(at[u], D)],
                                           start=True, stop=True)
                ins.then_inc(e_picked, 1)

            def total_group(g, h):
                if not isinstance(g, int) or g < 2 * TRIPS - 1:
                    pick_u(g + 1, 1 - h)
                pe.wait_ge(e_squared, g + 1)
                for u in range(GRP):
                    ins = nc.tensor.matmul(ps_stat[:, bass.ds(g, 1)], G[:, h, u, :],
                                           MASK[:, bass.ds(g * GRP + u, 1)], start=False, stop=False,
                                           skip_group_check=True)
                ins.then_inc(product[h], 1)
                pe.sem_inc(pe_go, 1)
            pick_u(0, 0)
            total_group(0, 0)
            with pe.Fori(0, TRIPS - 1) as i:
                total_group(2 * i + 1, 1)
                total_group(2 * i + 2, 0)
            total_group(2 * TRIPS - 1, 1)

            pe.wait_ge(stat_wide, 1)
            nc.tensor.matmul(ps[:, 0:P], TOTAL, IDENT[:, :], start=True, stop=True).then_inc(stat_sum, 1)

            pe.wait_ge(bn_ready, 1)

            def sum_group(g, h, i):
                base = 2048 + 1024 * h
                places = load_places(LOC, g, (GRP - 1) * D)
                if static(g, 2):
                    pe.wait_ge(group_added, LAST_PASS * GK + g)
                    pe.sem_inc(pe_go, 1)
                zero(base, GRP * D)
                pe.wait_ge(e_onehot, g + 1)
                pe.wait_ge(e_acted, g + 1)
                for u in range(GRP):
                    ins = accumulate(base, places[u], D, OH[:, h, u, :], ACTED[:, h, u, :])
                ins.then_inc(e_product, 1)
            groups_apart(pe, sum_group)

        @block.vector
        def _(dve):
            count = [0]

            def link(ins):
                count[0] += 1
                ins.then_inc(dve_done, 1)
                dve.wait_ge(dve_done, count[0])

            V = nc.vector

            V.memset(EPSC[:, :], EPS)
            V.memset(ZERO[:, :], 0.0)
            V.memset(ONE16[:, :], 1.0)
            V.memset(BG3[:, :], 0.0)
            V.memset(LOC[:, :], 0)
            V.memset(SLOT[:, :], 0)
            V.memset(ONES[:, :], 1.0)
            V.memset(XT[D:D + 1, :, :], 1.0)
            V.memset(R1[D:D + 1, :, :], 1.0)
            V.memset(WG[0:D, 3 * D:4 * D], 0.0)
            V.memset(WG[D:P, 2 * D:3 * D], 0.0)
            V.memset(BG[:, 0, 3 * D:4 * D], 0.0)
            V.memset(BG[:, 1, 2 * D:3 * D], 0.0)
            dve.wait_ge(iota_done, 4)
            V.tensor_scalar(IDENT[:, :], IOTAR[:, :], VIS[:, 0:1], None, ALU.is_equal)

            dve.wait_ge(ends_in, 16)
            link(V.tensor_copy(ENDF[:, :], ENDS[:, :]))
            link(V.tensor_tensor(BELOW[:, :, :], ENDF[:, :].unsqueeze(1).broadcast_to([P, NB, VT]),
                                 BND[:, :].unsqueeze(2).broadcast_to([P, NB, VT]), ALU.is_lt))
            V.tensor_reduce(CNTB[:, :], BELOW[:, :, :], AX_X, ALU.add).then_inc(below, 1)
            dve.wait_ge(totals, 1)
            link(V.tensor_tensor(TS[:, :], ps[:, 0:NB], IOB[:, :], ALU.add))
            for g in range(VT):
                link(V.tensor_scalar(CNTB[:, 0:NB - 1], TS[:, 0:NB - 1], VIS[:, g:g + 1], 0.0, ALU.is_le, ALU.add,
                                     accum_out=BJ[:, g:g + 1]))
            link(V.tensor_tensor(TJF[:, :], VIS[:, :], BJ[:, :], ALU.subtract))
            V.tensor_scalar(TJ[:, :], TJF[:, :], float(ROWS - 1), None, ALU.min).then_inc(rows_known, 1)
            link(V.tensor_scalar(BJ128[:, :], BJ[:, :], float(P), None, ALU.mult))

            def over_f(t):
                return t[:, :].unsqueeze(2).broadcast_to([P, NB, D])

            def over_b(k):
                return BC[:, k:k + 1, :].broadcast_to([P, NB, D])

            def centre():
                link(V.tensor_reduce(SA[:, :], X[:, :, :], AX_X, ALU.add))
                link(V.tensor_scalar(SA[:, :], SA[:, :], -1.0 / D, None, ALU.mult))
                V.tensor_tensor(H[:, :, :], X[:, :, :], over_f(SA), ALU.add).then_inc(centred, 1)

            def rescale(n, to, squares):
                dve.wait_ge(squared, n + 1)
                V.tensor_reduce(SA[:, :], squares, AX_X, ALU.add).then_inc(varred, 1)
                dve.wait_ge(rooted, n + 1)
                link(V.reciprocal(SB[:, :], SB[:, :]))
                V.scalar_tensor_tensor(to, H[:, :, :], 0.0, over_f(SB), ALU.max, ALU.mult).then_inc(normed, 1)

            def norm(n, to):
                centre()
                rescale(n, to, SUMS)

            dve.wait_ge(x_in, 16)
            centre()

            dve.wait_ge(typ_in, 32)
            V.tensor_scalar(RLO, SRC, P - 1, None, ALU.bitwise_and)
            link(V.tensor_scalar(RHI, SRC, 7, None, ALU.arith_shift_right))
            link(V.scalar_tensor_tensor(F3[:, 2, :, :], RLO, float(NB), RHI, ALU.mult, ALU.add))
            link(V.scalar_tensor_tensor(F3[:, 2, :, :], F3[:, 2, :, :], float(TYPES), TYP, ALU.mult, ALU.add))

            dve.wait_ge(rows_in, 16 * VT)
            for g in range(VT):
                V.tensor_scalar(F3[:, 0, g, :], EB[:, g, 0, :], BJ128[:, g:g + 1], None, ALU.subtract)
            V.tensor_scalar(SLO, EB[:, :, 1, :], P - 1, None, ALU.bitwise_and)
            link(V.tensor_scalar(SHI, EB[:, :, 1, :], 7, None, ALU.arith_shift_right))
            V.scalar_tensor_tensor(F3[:, 1, :, :], SLO, float(NB), SHI, ALU.mult, ALU.add).then_inc(cols_done, 1)

            def clear(view):
                V.memset(view, 0.0).then_inc(group_added, 1)

            def add_group(n, g, products_, width):
                b = dve.value_load(FIRST[0:1, bass.ds(g, 1)], min_val=0, max_val=NB - GRP)
                sums = A3[:, bass.ds(b, GRP), 0:width]
                dve.wait_ge(group_added, n * GK + g + 1)
                return V.tensor_tensor(sums, sums, products_[:, 0:GRP, 0:width], ALU.add).then_inc(group_added, 1)

            def onehots(cols, h):
                return V.tensor_tensor(OH[:, h, :, :], IOTAR[:, :].unsqueeze(1).broadcast_to([P, GRP, P]),
                                       cols.unsqueeze(2).broadcast_to([P, GRP, P]), ALU.is_equal)

            def sum_edges(n, width):
                for h in range(2):
                    onehots(group_cols(DLOC, 0, h), h).then_inc(onehot[h], 1)

                def add(i, h):
                    dve.wait_ge(product[h], n * TRIPS + i + 1)
                    dve.sem_inc(dve_go, 1)
                    add_group(n, 2 * i + h, ps_g[:, h, :, :], width)
                with dve.Fori(0, TRIPS - 1) as i:
                    for h in range(2):
                        add(i, h)
                        onehots(group_cols(DLOC, i + 1, h), h).then_inc(onehot[h], 1)
                for h in range(2):
                    add(TRIPS - 1, h)
                dve.wait_ge(group_added, (n + 1) * GK)

            rescale(0, H[:, :, :], SQ0)
            V.memset(G[:, :, :, D:D + 1], 1.0)
            dve.wait_ge(tabled, 4)
            dve.wait_ge(blk_in, 16)
            blk = BLK[:, 0:VISITS].rearrange("a (g u) -> a g u", u=GRP)
            batches = LOC[:, :].rearrange("a (g u) -> a g u", u=LPG)[:, :, GRP:GRP + 1]
            slot = SLOT[:, :].rearrange("a (g u) -> a g u", u=LPG)[:, :, 0:GRP]
            loc = LOC[:, :].rearrange("a (g u) -> a g u", u=LPG)[:, :, 0:GRP]
            first = FIRST[:, :].unsqueeze(2)
            link(V.tensor_scalar(first, blk[:, :, 0:1], (NB - GRP) * P, None, ALU.min))
            link(V.tensor_tensor(loc, blk, first.broadcast_to([1, 2 * TRIPS, GRP]), ALU.subtract))
            link(V.tensor_scalar(FIRST[:, :], FIRST[:, :], 7, None, ALU.arith_shift_right))
            dve.wait_ge(vnum_set, 1)
            link(V.tensor_scalar(VTMP, blk, 7, None, ALU.arith_shift_right))
            link(V.tensor_tensor(VROW, VNUM, VTMP, ALU.subtract))
            last = VROW[:, :, GRP - 1:GRP]
            link(V.tensor_scalar(batches, last, BATCH_OF[0], None, ALU.mult))
            link(V.tensor_scalar(batches, batches, BATCH_OF[1], None, ALU.arith_shift_right))
            link(V.tensor_scalar(batches, batches, 1, None, ALU.add))
            link(V.tensor_scalar(VTMP, VROW, LAP_OF[0], None, ALU.mult))
            link(V.tensor_scalar(VTMP, VTMP, LAP_OF[1], None, ALU.arith_shift_right))
            link(V.scalar_tensor_tensor(slot, VTMP, -float(RING_ROWS), VROW, ALU.mult, ALU.add))
            link(V.tensor_scalar(slot, slot, D, None, ALU.mult))
            clear(A3[:, :, 0:D + 1])
            dve.sem_inc(loc_set, 1)
            dve.wait_ge(dloc_out, 16)
            sum_edges(0, D + 1)
            V.tensor_copy(CNT[:, :].unsqueeze(2), A3[:, :, D:D + 1])
            dve.sem_inc(mlp_in, 1)

            def mlp_chunk(c, s, i):
                dve.wait_ge(chunk_made, RUN_MLP * NCH + c + 1)
                V.scalar_tensor_tensor(two(X, c), ps_x[:, s, :, :], 0.0, two(X, c), ALU.max, ALU.add
                                       ).then_inc(mlp_done, 1)
            chunks(dve, mlp_chunk)
            dve.wait_ge(mlp_done, NCH)

            total, rest = BG[:, 0, :], BG[:, 1, :]
            link(V.tensor_tensor(total, total, rest, ALU.add))
            for part in range(3):
                one = BG3[32 * part:32 * part + 1, :].rearrange("a (k f) -> a k f", k=CH)
                link(V.tensor_copy(one, total.unsqueeze(1).broadcast_to([1, CH, 4 * D])))
                if part < 2:
                    link(V.tensor_copy(rest, one[:, 0, :]))
                    link(V.tensor_tensor(total, total, rest, ALU.subtract))
            norm(1, FEAT)
            with dve.Fori(0, STEPS) as step:
                clear(SUMS)

                def type_chunk(c, s, i):
                    dve.wait_ge(chunk_made, (2 * step + RUN_TYPE) * NCH + c + 1)
                    if static(i):
                        dve.wait_ge(typ_out[s], step * SLOT_DMAS[s] + i * 16)
                    V.tensor_copy(TW[:, s, TYPES * D:], ps_m[:, s, 0:TYPES * D]).then_inc(typ_dve, 1)
                chunks(dve, type_chunk)
                sum_edges(step + 1, D)

                def gru_new(c, s, i):
                    done = step * (NCH * 2) + c * 2
                    dve.wait_ge(gru_sig, step * NCH + c + 1)
                    V.tensor_tensor(NN[:, s, :, :], RZ[:, s, :, 0:D], ps_gate[:, s, :, 3 * D:4 * D], ALU.mult
                                    ).then_inc(gru_pre, 1)
                    dve.wait_ge(gru_pre, done + 1)
                    V.tensor_tensor(NN[:, s, :, :], NN[:, s, :, :], ps_gate[:, s, :, 2 * D:3 * D], ALU.add
                                    ).then_inc(gru_pre, 1)

                def gru_mix(c, s, i):
                    done = step * (NCH * 3) + c * 3
                    feat, z = two(FEAT, c), RZ[:, s, :, D:2 * D]
                    dve.wait_ge(gru_tanh, step * NCH + c + 1)
                    V.tensor_tensor(DZ[:, s, :, :], feat, NN[:, s, :, :], ALU.subtract).then_inc(gru_out, 1)
                    dve.wait_ge(gru_out, done + 1)
                    V.tensor_tensor(DZ[:, s, :, :], DZ[:, s, :, :], z, ALU.mult).then_inc(gru_out, 1)
                    dve.wait_ge(gru_out, done + 2)
                    V.tensor_tensor(feat, NN[:, s, :, :], DZ[:, s, :, :], ALU.add).then_inc(gru_out, 1)
                chunks(dve, gru_new, gru_mix)
                dve.wait_ge(gru_out, (step + 1) * (NCH * 3))
            link(V.tensor_tensor(X[:, :, :], X[:, :, :], FEAT, ALU.add))

            V.tensor_scalar(IDX4[:, :], IDX4[:, :], 2, None, ALU.arith_shift_right).then_inc(idx_shifted, 1)
            norm(2, H[:, :, :])
            dve.wait_ge(root_deg, 1)
            link(V.reciprocal(DINV[:, :], SC[:, :]))
            for k in range(2):
                dve.sem_inc(gcn_in, 1)

                def gcn_chunk(c, s, i):
                    dve.wait_ge(chunk_made, (RUN_GCN + k) * NCH + c + 1)
                    scale = DINV[:, bass.ds(c * CH, CH)].unsqueeze(2).broadcast_to([P, CH, D])
                    V.tensor_tensor(two(SUMS, c), ps_x[:, s, :, :], scale, ALU.mult)
                    V.tensor_tensor(two(FEAT, c), ps_x[:, s, :, :], scale, ALU.mult).then_inc(gcn_done, 1)
                chunks(dve, gcn_chunk)
                dve.wait_ge(gcn_done, (k + 1) * NCH)
                dve.sem_inc(group_added, 1)
                sum_edges(STEPS + 1 + k, D)
                link(V.tensor_tensor(H[:, :, :], SUMS, over_f(DINV), ALU.mult))
                link(V.tensor_tensor(H[:, :, :], H[:, :, :], over_b(k), ALU.add))
                if k == 0:
                    link(V.tensor_scalar(H[:, :, :], H[:, :, :], 0.0, None, ALU.max))
                    dve.wait_ge(table_out, 16 + 16 * NCH)
                else:
                    link(V.tensor_tensor(X[:, :, :], X[:, :, :], H[:, :, :], ALU.add))

            link(V.tensor_tensor(W3[:, 1, :], W3A[:, :], W3[:, 0, :], ALU.subtract))
            norm(3, H[:, :, :])
            link(V.tensor_scalar(MASK, DLOC[:, :], 0.0, None, ALU.is_ge))
            link(V.scalar_tensor_tensor(MASK, DLOC[:, :], P - 0.5, MASK, ALU.is_lt, ALU.mult))
            loc_all = LOC[:, :].rearrange("a (g u) -> a g u", u=LPG)
            link(V.tensor_scalar(LOC[:, :], LOC[:, :], 1, None, ALU.arith_shift_right))
            V.scalar_tensor_tensor(AT.rearrange("a (g u) -> a g u", u=LPG), first.broadcast_to([1, 2 * TRIPS, LPG]),
                                   float(D), loc_all, ALU.mult, ALU.add).then_inc(mask_set, 1)

            def edge_chunk(c, s, i):
                dve.wait_ge(chunk_made, RUN_EDGE * NCH + c + 1)
                if static(i):
                    dve.wait_ge(edg_out[s], i * 16)
                V.tensor_copy(tw_v[:, s, :, :], ps_vu[:, s, :, 0:D]).then_inc(edg_v, 1)
                V.tensor_copy(two(H, c), ps_vu[:, s, :, D:P]).then_inc(edg_u, 1)
            chunks(dve, edge_chunk)

            def turned_onehots(g, h, i):
                dve.wait_ge(drow_in[h], i * 16 + 16)
                if static(g, 2):
                    dve.wait_ge(e_picked, g - 1)
                V.tensor_scalar(OTS[:, h, :, :], DROW[:, h, :, :], VIS[:, 0:1], None, ALU.is_equal
                                ).then_inc(e_turned, 1)

            def join(g, h, i):
                dve.wait_ge(e_picked, g + 1)
                dve.wait_ge(rows_other[h], rows_before(2, h, 1) + (i + 1) * (16 * GRP))
                V.tensor_tensor(G[:, h, :, 0:D], G[:, h, :, 0:D], ps_u[:, h, 0:GRP, :], ALU.add).then_inc(e_joined, 1)

            turned_onehots(0, 0, 0)
            turned_onehots(1, 1, 0)
            join(0, 0, 0)
            with dve.Fori(1, TRIPS) as i:
                turned_onehots(2 * i, 0, i)
                join(2 * i - 1, 1, i - 1)
                turned_onehots(2 * i + 1, 1, i)
                join(2 * i, 0, i)
            join(2 * TRIPS - 1, 1, TRIPS - 1)

            bias, gamma, beta = (BC[:, k, :] for k in (2, 3, 4))
            for h in range(2):
                dve.wait_ge(product[h], (LAST_PASS + 1) * TRIPS)
            link(V.tensor_reduce(SB[:, 0:STAT // STAT_CH], ps_stat.rearrange("p (a b) -> p a b", b=STAT_CH), AX_X,
                                 ALU.add))
            link(V.tensor_reduce(SA[:, 0:1], SB[:, 0:STAT // STAT_CH], AX_X, ALU.add))
            V.tensor_copy(TOTAL, SA[:, 0:1].broadcast_to([P, P])).then_inc(stat_wide, 1)
            dve.wait_ge(stat_sum, 1)
            link(V.tensor_scalar(ST[:, S_MEAN, :], ps[:, 0:D], 1.0 / E, None, ALU.mult))
            link(V.tensor_scalar(ST[:, S_VAR, :], ps[:, D:2 * D], 1.0 / E, None, ALU.mult))
            link(V.tensor_tensor(ST[:, S_TMP, :], ST[:, S_MEAN, :], ST[:, S_MEAN, :], ALU.mult))
            link(V.tensor_tensor(ST[:, S_VAR, :], ST[:, S_VAR, :], ST[:, S_TMP, :], ALU.subtract))
            V.tensor_scalar(ST[:, S_VAR, :], ST[:, S_VAR, :], 0.0, None, ALU.max).then_inc(stat_var, 1)
            link(V.tensor_tensor(ST[:, S_MEAN, :], ST[:, S_MEAN, :], bias, ALU.add))
            dve.wait_ge(stat_root, 1)
            link(V.reciprocal(ST[:, S_SCALE, :], ST[:, S_ROOT, :]))
            link(V.tensor_tensor(ST[:, S_SCALE, :], ST[:, S_SCALE, :], gamma, ALU.mult))
            link(V.tensor_tensor(ST[:, S_SHIFT, :], bias, ST[:, S_MEAN, :], ALU.subtract))
            link(V.tensor_tensor(ST[:, S_SHIFT, :], ST[:, S_SHIFT, :], ST[:, S_SCALE, :], ALU.mult))
            link(V.tensor_tensor(ST[:, S_SHIFT, :], ST[:, S_SHIFT, :], beta, ALU.add))
            dve.sem_inc(bn_ready, 1)
            clear(SUMS)

            def edge_onehots(g, h):
                onehots(DLOC[:, bass.ds(g * GRP, GRP)], h).then_inc(e_onehot, 1)

            def edge_act(g, h, i):
                dve.wait_ge(e_scaled, g + 1)
                if static(g, 2):
                    dve.wait_ge(e_product, g - 1)
                scaled = SCALED[:, h, :, :]
                V.scalar_tensor_tensor(ACTED[:, h, :, :], scaled, SLOPE, scaled, ALU.mult, ALU.max
                                       ).then_inc(e_acted, 1)

            def edge_add(g, h):
                dve.wait_ge(e_product, g + 1)
                dve.sem_inc(dve_go, 1)
                add_group(LAST_PASS, g, ps_s[:, h, :, :], D)

            for h in range(2):
                edge_onehots(h, h)
                edge_act(h, h, 0)
            with dve.Fori(1, TRIPS) as i:
                for h in range(2):
                    edge_add(2 * i + (h - 2), h)
                    edge_onehots(2 * i + h, h)
                    edge_act(2 * i + h, h, i)
            for h in range(2):
                edge_add(2 * TRIPS - 2 + h, h)
            dve.wait_ge(group_added, (LAST_PASS + 1) * GK)

            link(V.tensor_scalar(CNT[:, :], CNT[:, :], 1.0, None, ALU.max))
            link(V.reciprocal(CNT[:, :], CNT[:, :]))
            link(V.tensor_tensor(H[:, :, :], SUMS, over_f(CNT), ALU.mult))
            V.tensor_tensor(X[:, :, :], X[:, :, :], H[:, :, :], ALU.add).then_inc(result, 1)


def kernel(**inputs):
    import numpy as np
    import concourse.bacc as bacc
    from concourse.bass_utils import run_bass_kernel_spmd

    a = {k: np.asarray(v) for k, v in inputs.items()}
    xp = np.zeros((NB * P, D), np.float32)
    xp[:N] = a["x"]
    edges = np.zeros((3, VT * P * P), np.int32)
    edges[0, E:] = FAR
    for k, name in enumerate(("dst", "src", "edge_type_4")):
        edges[k, :E] = a[name]
    arrays = {
        "x": np.ascontiguousarray(xp.reshape(NB, P, D).transpose(1, 0, 2)),
        "edges": np.ascontiguousarray(edges.reshape(3, VT * P, P).transpose(1, 0, 2)).reshape(VT * P, 3 * P),
        "row_ends": edges[0, P - 1::P].reshape(P, VT),
        "L0_W1": a["L0_gnn_W1"], "L0_b1": a["L0_gnn_b1"], "L0_W2": a["L0_gnn_W2"], "L0_b2": a["L0_gnn_b2"],
        "L1_Wt": a["L1_gnn_W"].transpose(2, 0, 1).reshape(D, TYPES * D), "L1_b": a["L1_gnn_b"].reshape(1, TYPES * D),
        "L1_wih": a["L1_gnn_w_ih"].T, "L1_whh": a["L1_gnn_w_hh"].T,
        "L1_bih": a["L1_gnn_b_ih"].reshape(1, 3 * D), "L1_bhh": a["L1_gnn_b_hh"].reshape(1, 3 * D),
        "L2_W1": a["L2_gnn_W1"], "L2_b1": a["L2_gnn_b1"], "L2_W2": a["L2_gnn_W2"], "L2_b2": a["L2_gnn_b2"],
        "L3_Wt": a["L3_gnn_W"].T, "L3_b": a["L3_gnn_b"], "L3_gamma": a["L3_gnn_gamma"], "L3_beta": a["L3_gnn_beta"],
    }
    arrays = {k: np.ascontiguousarray(v) for k, v in arrays.items()}
    nc = bacc.Bacc("TRN2", target_bir_lowering=False, num_devices=1)
    args = {k: nc.dram_tensor(k, v.shape, mybir.dt.from_np(v.dtype), kind="ExternalInput").ap()
            for k, v in arrays.items()}
    out = nc.dram_tensor("out", (P, NB, D), F32, kind="ExternalOutput").ap()
    gnn_kernel(nc, out=out, **args)
    r = run_bass_kernel_spmd(nc, [arrays], core_ids=[0])
    return r.results[0]["out"].transpose(1, 0, 2).reshape(NB * P, D)[:N]
```
